# Optimizing a Trainium2 kernel written in Bass

```python
import numpy as np
import jax
import jax.numpy as jnp

def _softmax(x, axis=-1):
    return jax.nn.softmax(x, axis=axis)

def _gelu(x):
    return jax.nn.gelu(x, approximate=True)

def _silu(x):
    return jax.nn.silu(x)

def _sigmoid(x):
    return jax.nn.sigmoid(x)

def _layernorm(x, axis=-1, eps=1e-05):
    m = jnp.mean(x, axis=axis, keepdims=True)
    v = jnp.var(x, axis=axis, keepdims=True)
    return (x - m) / jnp.sqrt(v + eps)

def _scatter_add(tgt, idx, src, axis=0):
    return tgt.at[idx].add(src)

def _segment_sum(src, seg, n):
    return jax.ops.segment_sum(src, seg, n)
kernel_name = 'mk_seq_postln_d1_jaxref_r4_32d902'

def setup_inputs(seed: int=0):
    np.random.seed(seed)
    _w = jnp.asarray

    def _L0_attn_setup():
        import jax, jax.numpy as jnp
        import numpy as np
        B, N, D_IN, D_OUT, HEADS = (4, 1024, 256, 256, 16)
        D_HEAD = D_OUT // HEADS
        key = jax.random.key(seed)
        ks = jax.random.split(key, 5)
        x = jax.random.normal(ks[0], (B, N, D_IN), dtype=jnp.float32)
        s_in = 1.0 / np.sqrt(D_IN)
        s_out = 1.0 / np.sqrt(D_OUT)
        Wq = jax.random.normal(ks[1], (D_IN, D_OUT), dtype=jnp.float32) * s_in
        Wk = jax.random.normal(ks[2], (D_IN, D_OUT), dtype=jnp.float32) * s_in
        Wv = jax.random.normal(ks[3], (D_IN, D_OUT), dtype=jnp.float32) * s_in
        Wo = jax.random.normal(ks[4], (D_OUT, D_OUT), dtype=jnp.float32) * s_out
        bo = jnp.zeros((D_OUT,), dtype=jnp.float32)
        return {'x': x, 'Wq': Wq, 'Wk': Wk, 'Wv': Wv, 'Wo': Wo, 'bo': bo}
    _L0_attn_in = _L0_attn_setup()

    def _L0_ffn_setup():
        import jax, jax.numpy as jnp
        import numpy as np
        TOP_K = 2
        CAP_FACTOR = 1.25

        def _gelu(x):
            return 0.5 * x * (1.0 + jnp.tanh(jnp.sqrt(2.0 / jnp.pi) * (x + 0.044715 * x ** 3)))
        key = jax.random.key(seed)
        ks = jax.random.split(key, 6)
        B, S, D, F, E = (4, 512, 256, 1024, 8)
        return {'hidden_states': jax.random.normal(ks[0], (B, S, D), dtype=jnp.float32), 'wr': jax.random.normal(ks[1], (E, D), dtype=jnp.float32) * 0.02, 'w1': jax.random.normal(ks[2], (E, D, F), dtype=jnp.float32) * 0.02, 'b1': jnp.zeros((E, F), dtype=jnp.float32), 'w2': jax.random.normal(ks[3], (E, F, D), dtype=jnp.float32) * 0.02, 'b2': jnp.zeros((E, D), dtype=jnp.float32)}
    _L0_ffn_in = _L0_ffn_setup()
    _d = {'L0_attn_x': _L0_attn_in['x'], 'L0_attn_Wq': _L0_attn_in['Wq'], 'L0_attn_Wk': _L0_attn_in['Wk'], 'L0_attn_Wv': _L0_attn_in['Wv'], 'L0_attn_Wo': _L0_attn_in['Wo'], 'L0_attn_bo': _L0_attn_in['bo'], 'L0_ffn_wr': _L0_ffn_in['wr'], 'L0_ffn_w1': _L0_ffn_in['w1'], 'L0_ffn_b1': _L0_ffn_in['b1'], 'L0_ffn_w2': _L0_ffn_in['w2'], 'L0_ffn_b2': _L0_ffn_in['b2']}
    _x0 = _d['L0_attn_x']
    _d['L0_attn_x'] = jax.random.normal(jax.random.fold_in(jax.random.key(seed), 1), (16, 1024, 256), dtype=_x0.dtype)
    del _x0
    return _d

def reference(L0_attn_x, L0_attn_Wq, L0_attn_Wk, L0_attn_Wv, L0_attn_Wo, L0_attn_bo, L0_ffn_wr, L0_ffn_w1, L0_ffn_b1, L0_ffn_w2, L0_ffn_b2):

    def _L0_attn_ref(x, Wq, Wk, Wv, Wo, bo):
        import jax, jax.numpy as jnp
        import numpy as np
        B, N, D_IN, D_OUT, HEADS = (4, 1024, 256, 256, 16)
        D_HEAD = D_OUT // HEADS
        q = jax.nn.softmax(jnp.einsum('bni,io->bno', x, Wq), axis=-1)
        k = jax.nn.softmax(jnp.einsum('bni,io->bno', x, Wk), axis=-2)
        v = jnp.einsum('bni,io->bno', x, Wv)
        scale = 1.0 / np.sqrt(D_HEAD).astype(np.float32)
        ctx = jnp.einsum('bnd,bne->bde', k, v) * scale
        y = jnp.einsum('bnd,bde->bne', q, ctx) / jnp.float32(D_OUT)
        return jnp.einsum('bnd,de->bne', y, Wo) + bo

    def _L0_ffn_ref(hidden_states, wr, w1, b1, w2, b2):
        import jax, jax.numpy as jnp
        import numpy as np
        TOP_K = 2
        CAP_FACTOR = 1.25

        def _gelu(x):
            return 0.5 * x * (1.0 + jnp.tanh(jnp.sqrt(2.0 / jnp.pi) * (x + 0.044715 * x ** 3)))
        B, S, D = hidden_states.shape
        E = wr.shape[0]
        x = hidden_states.reshape(-1, D)
        T = x.shape[0]
        logits = x @ wr.T
        vals, idx = jax.lax.top_k(logits, TOP_K)
        sparse = jnp.full((T, E), -jnp.inf, dtype=logits.dtype)
        sparse = sparse.at[jnp.arange(T)[:, None], idx].set(vals)
        gating = jax.nn.softmax(sparse, axis=-1)
        cap = max(8, int(max(1, T * TOP_K // E) * CAP_FACTOR))
        mask = (idx[:, :, None] == jnp.arange(E)).any(axis=1)
        pos = jnp.cumsum(mask.astype(jnp.int32), axis=0) - 1
        keep = mask & (pos < cap)
        slot = jnp.where(keep, pos, cap)
        e_grid = jnp.broadcast_to(jnp.arange(E)[None, :], (T, E))
        t_grid = jnp.broadcast_to(jnp.arange(T)[:, None], (T, E))
        dispatch = jnp.full((E, cap + 1), T, dtype=jnp.int32)
        dispatch = dispatch.at[e_grid, slot].set(t_grid)[:, :cap]
        x_pad = jnp.concatenate([x, jnp.zeros((1, D), x.dtype)], axis=0)
        g_pad = jnp.concatenate([gating, jnp.zeros((1, E), gating.dtype)], axis=0)
        xg = x_pad[dispatch]
        h = _gelu(jnp.einsum('ecd,edf->ecf', xg, w1) + b1[:, None, :])
        y = jnp.einsum('ecf,efd->ecd', h, w2) + b2[:, None, :]
        g = g_pad[dispatch, jnp.arange(E)[:, None]]
        wy = y * g[..., None]
        out = jax.ops.segment_sum(wy.reshape(-1, D), dispatch.reshape(-1), num_segments=T + 1)[:T]
        return out.reshape(B, S, D)
    x = L0_attn_x
    x = _layernorm(x + _L0_attn_ref(x, L0_attn_Wq, L0_attn_Wk, L0_attn_Wv, L0_attn_Wo, L0_attn_bo), axis=-1)
    x = _layernorm(x + _L0_ffn_ref(x, L0_ffn_wr, L0_ffn_w1, L0_ffn_b1, L0_ffn_w2, L0_ffn_b2), axis=-1)
    return x

_drawn_inputs = setup_inputs


def setup_inputs(seed=0):
    import zlib

    import numpy as np

    out = dict(_drawn_inputs(seed))
    spreads = {'L0_attn_bo': (0.0, 0.1), 'L0_ffn_b1': (0.0, 0.306), 'L0_ffn_b2': (0.0, 0.1)}
    factors = {'L0_attn_Wq': 8.0, 'L0_attn_Wk': 8.0, 'L0_attn_Wv': 8.0, 'L0_attn_Wo': 8.0}
    for name, (base, spread) in spreads.items():
        noise = np.random.default_rng([zlib.crc32(name.encode()), seed]).standard_normal(out[name].shape)
        drawn = base * np.exp(spread * noise) if base else spread * noise
        out[name] = jnp.asarray(drawn.astype(out[name].dtype))
    for name, factor in factors.items():
        out[name] = (out[name] * factor).astype(out[name].dtype)
    return out
```

```python
import numpy as np
import concourse.bass as bass
from concourse import mybir
from contextlib import ExitStack


def build(nc, x, x_t, wq, wk, wv_t, wo, bo, wr_t, w1, b1_t, w2, b2_t, out):
    F = mybir.dt.float32
    R = mybir.dt.float32r
    I = mybir.dt.int32
    ALU = mybir.AluOpType
    ACT = mybir.ActivationFunctionType
    X = mybir.AxisListType.X

    NB, N, D = x.shape
    E, _, FF = w1.shape
    P = 128
    T = NB * N
    TILES = N // P
    PAIRS = TILES // 2
    DK = D // P
    FT = FF // P
    CAP = max(8, int(T * 2 // E * 1.25))
    SLOTS = E * CAP
    TCOLS = SLOTS // P
    BLK = 512
    BT = BLK // P
    BLOCKS = CAP // BLK
    HEADS = 16
    CTX_SCALE = 1.0 / float(np.sqrt(D // HEADS)) / D
    EPS = 1e-5
    DROPPED = float(2 ** 23)
    assert CAP % (2 * BLK) == 0 and NB % 2 == 0 and E % 2 == 0 and TILES == 8 and DK == 2 and FT == 8

    x_rows = x.rearrange("b (p t) d -> b p (t d)", t=TILES)
    xt_rows = x_t.rearrange("b (k p) n -> b p k n", p=P)
    x1_dram = nc.dram_tensor("x1_rows", (T + BLK, D), F, kind="Internal").ap()
    acc_dram = nc.dram_tensor("sum_rows", (T + BLK, D), F, kind="Internal").ap()
    table_dram = nc.dram_tensor("slot_table", (SLOTS, 2), I, kind="Internal").ap()
    x1_store = x1_dram[0:T, :].rearrange("(b p t) d -> b p (t d)", p=P, t=TILES)
    acc_store = acc_dram[0:T, :].rearrange("(b p t) d -> b p (t d)", p=P, t=TILES)
    out_store = out.rearrange("b (p t) d -> b p (t d)", t=TILES)
    table_rows = table_dram.rearrange("(p c) w -> p (c w)", p=P)

    outer = ExitStack()
    with outer:
        def sem(name):
            return outer.enter_context(nc.semaphore(name))

        def sems(name, n):
            return [sem(f"{name}{i}") for i in range(n)]

        apart = sem("apart")

        def wait_apart(eng, which, value):
            eng.wait_ge(which, value)
            eng.sem_inc(apart, 1)

        def keep(name, shape, dt=F):
            return outer.enter_context(nc.sbuf_tensor(name, shape, dt))

        ident = keep("ident", [P, P])
        w_raw = keep("w_raw", [P, 2 * DK * FF])
        w_hi = [keep("w_hi0", [P, 2 * DK * FF], R), None]
        w_lo = [keep("w_lo0", [P, 2 * DK * FF], R), None]
        b1_sb = keep("b1_sb", [P, E * FT])
        b2_sb = keep("b2_sb", [P, E * DK])
        W1 = DK * FF

        w_loaded = sem("w_loaded")
        w_split = sem("w_split")
        bias_loaded = sem("bias_loaded")

        def load_expert(sp, e):
            sp.dma_start(w_raw[:, 0:W1].rearrange("p (k f) -> p k f", k=DK),
                         w1[e, :, :].rearrange("(k p) f -> p k f", p=P)).then_inc(w_loaded, 16)
            sp.dma_start(w_raw[:, W1:2 * W1].rearrange("p (k d) -> p k d", k=FT),
                         w2[e, :, :].rearrange("(k p) d -> p k d", p=P)).then_inc(w_loaded, 16)

        with ExitStack() as phase:
            def sb(name, shape, dt=F):
                return phase.enter_context(nc.sbuf_tensor(name, shape, dt))

            def ps(name, shape):
                return phase.enter_context(nc.psum_tensor(name, shape, F))

            x_raw = [sb(f"x_raw{i}", [P, TILES, D]) for i in range(2)]
            xt_raw = [sb(f"xt_raw{i}", [P, DK * N]) for i in range(2)]
            x_hi, x_lo = sb("x_hi", [P, TILES, D], R), sb("x_lo", [P, TILES, D], R)
            xt_hi, xt_lo = sb("xt_hi", [P, DK * N], R), sb("xt_lo", [P, DK * N], R)
            wq_hi, wq_lo = sb("wq_hi", [P, DK, D], R), sb("wq_lo", [P, DK, D], R)
            wk_hi, wk_lo = sb("wk_hi", [P, DK, D], R), sb("wk_lo", [P, DK, D], R)
            wvo_hi, wvo_lo = sb("wvo_hi", [P, DK, D], R), sb("wvo_lo", [P, DK, D], R)
            wr_sb = sb("wr_sb", [P, DK, E])
            bo_sb = sb("bo_sb", [P, D])
            k_exp = sb("k_exp", [P, DK, N])
            q_exp = sb("q_exp", [P, TILES, D])
            kt_hi, kt_lo = sb("kt_hi", [P, 2, 512], R), sb("kt_lo", [P, 2, 512], R)
            qt_hi, qt_lo = sb("qt_hi", [P, 2, 512], R), sb("qt_lo", [P, 2, 512], R)
            g_hi, g_lo = sb("g_hi", [P, DK, D], R), sb("g_lo", [P, DK, D], R)
            m_raw = sb("m_raw", [P, DK, D])
            m_hi, m_lo = sb("m_hi", [P, DK, D], R), sb("m_lo", [P, DK, D], R)
            r_sb = sb("r_sb", [P, TILES, D])
            x1_sb = [sb(f"x1_sb{i}", [P, TILES, D]) for i in range(2)]
            x1t = sb("x1t", [P, 2, 512])
            nk_max = sb("nk_max", [P, 2, DK])
            nq_max = sb("nq_max", [P, 2, TILES])
            zk, zq = sb("zk", [P, 2, DK]), sb("zq", [P, 2, TILES])
            rzk, rzq = sb("rzk", [P, DK]), sb("rzq", [P, TILES])
            stats = sb("stats", [P, TILES, 6])
            mean_var = sb("mean_var", [P, TILES, 2])
            rstd, nshift = sb("rstd", [P, TILES]), sb("nshift", [P, TILES])
            minus_half = sb("minus_half", [P, TILES])
            tri_f, ones_f = sb("tri_f", [P, P]), sb("ones_f", [P, P])
            ident_r, tri_r, ones_r = sb("ident_r", [P, P], R), sb("tri_r", [P, P], R), sb("ones_r", [P, P], R)
            logits = sb("logits", [P, TILES, E])
            second = sb("second", [P, TILES, E])
            eq = sb("eq", [P, TILES, E])
            score = sb("score", [P, TILES, E])
            pick = [sb(f"pick{i}", [P, TILES, E]) for i in range(2)]
            top = sb("top", [P, 2, TILES])
            best = sb("best", [P, TILES])
            mask = sb("mask", [P, TILES, E], R)
            mask_sum_f, mask_sum = sb("mask_sum_f", [P, E]), sb("mask_sum", [P, E], R)
            rank_base = sb("rank_base", [P, E])
            slot = sb("slot", [P, TILES, E])
            late = sb("late", [P, TILES, E])
            slot_f, slot_i = sb("slot_f", [P, 2, TILES]), sb("slot_i", [P, 2, TILES], I)
            slot_p, slot_c = sb("slot_p", [P, 2, TILES], I), sb("slot_c", [P, 2, TILES], I)
            gap, gap_exp = sb("gap", [P, TILES]), sb("gap_exp", [P, TILES])
            gate_sum = sb("gate_sum", [P, TILES])
            gates = sb("gates", [P, 2, TILES])
            token_id = sb("token_id", [P, TILES], I)
            order_w = sb("order_w", [P, E])
            slot_base = sb("slot_base", [P, E])
            ints = sb("ints", [P, 2, E], I)
            where = [sb(f"where{i}", [P, 2, TILES], I) for i in range(2)]
            entry = [sb(f"entry{i}", [P, 2, TILES, 2], I) for i in range(2)]
            pad_entries = sb("pad_entries", [P, TCOLS, 2], I)
            zero_rows = sb("zero_rows", [P, D])
            w_in = x1_sb[1][:, :, :].rearrange("p (i k) d -> p i (k d)", i=4)

            k_ps = ps("k_ps", [P, DK, N])
            g_ps = k_ps[:, 0, :].rearrange("p (k n) -> p k n", k=DK)[:, :, 0:D]
            m_ps = k_ps[:, 1, 0:2 * D].rearrange("p (k n) -> p k n", k=DK)
            l_ps = k_ps[:, 1, 512:512 + TILES * E].rearrange("p (t e) -> p t e", e=E)
            rank_ps = k_ps[:, 1, 640:640 + TILES * E].rearrange("p (t e) -> p t e", e=E)
            total_ps = k_ps[:, 1, 768:768 + E]
            qo_ps = ps("qo_ps", [P, 2, 512])
            t_ps = ps("t_ps", [P, 2, 512])

            consts_loaded = sem("consts_loaded")
            consts_made = sem("consts_made")
            consts_split = sem("consts_split")
            wvo_ready = sem("wvo_ready")
            pads_made, pads_stored = sem("pads_made"), sem("pads_stored")
            x_loaded, xt_loaded = sems("x_loaded", 2), sems("xt_loaded", 2)
            x_hi_done, x_lo_done = sem("x_hi_done"), sem("x_lo_done")
            xt_hi_done, xt_lo_done = sem("xt_hi_done"), sem("xt_lo_done")
            k_ready, k_max_done, k_exp_done = sem("k_ready"), sem("k_max_done"), sem("k_exp_done")
            q_ready, q_max_done, q_exp_done = sem("q_ready"), sem("q_max_done"), sem("q_exp_done")
            z_done = sem("z_done")
            kt_ready, kt_hi_done, kt_lo_done, kt_used = sem("kt_ready"), sem("kt_hi_done"), sem("kt_lo_done"), sem("kt_used")
            qt_ready, qt_hi_done, qt_lo_done = sem("qt_ready"), sem("qt_hi_done"), sem("qt_lo_done")
            g_hi_done, g_lo_done = sem("g_hi_done"), sem("g_lo_done")
            m_ready, m_raw_done, m_hi_done, m_lo_done = sem("m_ready"), sem("m_raw_done"), sem("m_hi_done"), sem("m_lo_done")
            o_ready, r_done, stats_done, mean_done = sem("o_ready"), sem("r_done"), sem("stats_done"), sem("mean_done")
            norm_step, norm_ready = sem("norm_step"), sem("norm_ready")
            x1_done, x1_stored = sem("x1_done"), sems("x1_stored", 2)
            x1t_ready, x1t_done = sem("x1t_ready"), sem("x1t_done")
            logits_ready, mask_ready, rank_ready = sem("logits_ready"), sem("mask_ready"), sem("rank_ready")
            gap_ready, gap_exp_done = sem("gap_ready"), sem("gap_exp_done")
            route_step, slots_ready = sem("route_step"), sem("slots_ready")
            entries_written = sems("entries_written", 2)
            const_step = sem("const_step")

            def batches(eng, body, peeled=1):
                for pair in range(peeled):
                    for u in range(2):
                        body(pair, u, pair == 0 and u == 0, False)
                with eng.Fori(peeled, NB // 2 - 1) as pair:
                    for u in range(2):
                        body(pair, u, False, False)
                for u in range(2):
                    body(NB // 2 - 1, u, False, u == 1)

            block_a = phase.enter_context(nc.Block())

            @block_a.sync
            def _(sp):
                sp.dma_start(xt_raw[0][:, :].rearrange("p (k n) -> p k n", k=DK), xt_rows[0]).then_inc(xt_loaded[0], 16)
                for i, w in enumerate((wk, wq, wv_t, wo)):
                    sp.dma_start(w_in[:, i, :].rearrange("p (k d) -> p k d", k=DK),
                                 w.rearrange("(k p) d -> p k d", p=P)).then_inc(consts_loaded, 16)
                sp.dma_start(wr_sb[:, :, :], wr_t.rearrange("(k p) e -> p k e", p=P)).then_inc(consts_loaded, 16)
                sp.dma_start(bo_sb[:, :], bo.rearrange("(a d) -> a d", a=1).broadcast_to([P, D])).then_inc(consts_loaded, 16)
                sp.dma_start(x_raw[0][:, :, :].rearrange("p t d -> p (t d)"), x_rows[0]).then_inc(x_loaded[0], 16)
                sp.dma_start(xt_raw[1][:, :].rearrange("p (k n) -> p k n", k=DK), xt_rows[1]).then_inc(xt_loaded[1], 16)
                sp.dma_start(x_raw[1][:, :, :].rearrange("p t d -> p (t d)"), x_rows[1]).then_inc(x_loaded[1], 16)
                sp.wait_ge(pads_made, 2)
                sp.dma_start(table_rows, pad_entries[:, :, :].rearrange("p c w -> p (c w)")).then_inc(pads_stored, 16)
                for rows_dram in (x1_dram, acc_dram):
                    for t in range(BT):
                        sp.dma_start(rows_dram[T + t * P:T + (t + 1) * P, :], zero_rows[:, :]).then_inc(pads_stored, 16)
                load_expert(sp, 0)
                sp.dma_start(b1_sb[:, :], b1_t).then_inc(bias_loaded, 16)
                sp.dma_start(b2_sb[:, :], b2_t).then_inc(bias_loaded, 16)

                def body(pair, u, first, last, more=True):
                    b = pair * 2 + u
                    sp.wait_ge(x1_done, b + 1)
                    sp.dma_start(x1_store[b], x1_sb[u][:, :, :].rearrange("p t d -> p (t d)")).then_inc(x1_stored[u], 16)
                    sp.dma_start(acc_store[b], x1_sb[u][:, :, :].rearrange("p t d -> p (t d)")).then_inc(x1_stored[u], 16)
                    if more:
                        sp.wait_ge(r_done, (b + 1) * TILES)
                        sp.wait_ge(x_lo_done, b + 1)
                        sp.dma_start(x_raw[u][:, :, :].rearrange("p t d -> p (t d)"), x_rows[b + 2]).then_inc(x_loaded[u], 16)
                        sp.wait_ge(xt_lo_done, b + 1)
                        sp.dma_start(xt_raw[u][:, :].rearrange("p (k n) -> p k n", k=DK), xt_rows[b + 2]).then_inc(xt_loaded[u], 16)

                with sp.Fori(0, NB // 2 - 1) as pair:
                    for u in range(2):
                        body(pair, u, False, False)
                for u in range(2):
                    body(NB // 2 - 1, u, False, True, more=False)
                for u in range(2):
                    sp.wait_ge(x1_stored[u], 32 * (NB // 2))
                sp.wait_ge(pads_stored, 16 * (1 + 2 * BT))
                sp.wait_ge(bias_loaded, 32)

            @block_a.gpsimd
            def _(pool):
                count = [0]

                def made(ins):
                    count[0] += 1
                    ins.then_inc(const_step, 1)
                    pool.wait_ge(const_step, count[0])

                nc.gpsimd.memset(minus_half[:, :], -0.5)
                made(nc.gpsimd.memset(ident[:, :], 0.0))
                made(nc.gpsimd.affine_select(out=ident[:, :], in_=ident[:, :], compare_op=ALU.not_equal, fill=1.0,
                                             base=0, pattern=[[-1, P]], channel_multiplier=1))
                made(nc.gpsimd.memset(tri_f[:, :], 0.0))
                made(nc.gpsimd.affine_select(out=tri_f[:, :], in_=tri_f[:, :], compare_op=ALU.is_ge, fill=1.0,
                                             base=0, pattern=[[-1, P]], channel_multiplier=1))
                made(nc.gpsimd.memset(ones_f[:, :], 1.0))
                made(nc.gpsimd.memset(rank_base[:, :], 0.0))
                made(nc.gpsimd.iota(ints[:, 0, :], pattern=[[-1, E]], base=E, channel_multiplier=0))
                made(nc.gpsimd.iota(ints[:, 1, :], pattern=[[CAP, E]], base=0, channel_multiplier=0))
                made(nc.gpsimd.iota(token_id[:, :], pattern=[[1, TILES]], base=0, channel_multiplier=TILES))
                made(nc.gpsimd.tensor_copy(order_w[:, :], ints[:, 0, :]))
                made(nc.gpsimd.tensor_copy(slot_base[:, :], ints[:, 1, :]))
                nc.gpsimd.memset(zero_rows[:, :], 0.0).then_inc(pads_made, 1)
                made(nc.gpsimd.memset(pad_entries[:, :, :], 0))
                nc.gpsimd.iota(pad_entries[:, :, 0].rearrange("p (a t) -> p a t", t=BT), pattern=[[0, TCOLS // BT], [P, BT]], base=T, channel_multiplier=1).then_inc(pads_made, 1)
                nc.gpsimd.memset(best[:, :], 0.0).then_inc(consts_made, 1)

                def split_x(b, u, loads):
                    pool.wait_ge(x_hi_done, b + 1)
                    nc.gpsimd.tensor_tensor(x_lo[:, :, :], x_raw[u][:, :, :], x_hi[:, :, :].bitcast(F),
                                            ALU.subtract).then_inc(x_lo_done, 1)

                def scatter(b_prev, u_prev):
                    wait_apart(pool, slots_ready, b_prev + 1)
                    for t in range(TILES):
                        for c in range(2):
                            pool.indirect_dma_start(
                                out=table_dram, out_offset=bass.IndirectOffsetOnAxis(ap=where[u_prev][:, c, t:t + 1], axis=0),
                                in_=entry[u_prev][:, c, t, :], in_offset=None,
                                bounds_check=SLOTS - 1, oob_is_err=False).then_inc(entries_written[u_prev], 16)

                split_x(0, 0, 1)
                pool.wait_ge(pads_stored, 16 * (1 + 2 * BT))

                def body(pair, u, first, last):
                    b = pair * 2 + u
                    if not last:
                        split_x(b + 1, 1 - u, None)
                    if not first:
                        pool.wait_ge(x1_done, b)
                    wait_apart(pool, mean_done, b + 1)
                    nc.gpsimd.tensor_scalar(rstd[:, :], mean_var[:, :, 1], EPS, None, ALU.add).then_inc(norm_step, 1)
                    pool.wait_ge(norm_step, 3 * b + 1)
                    nc.gpsimd.tensor_tensor(rstd[:, :], rstd[:, :], minus_half[:, :], ALU.pow).then_inc(norm_step, 1)
                    pool.wait_ge(norm_step, 3 * b + 2)
                    nc.gpsimd.tensor_tensor(nshift[:, :], mean_var[:, :, 0], rstd[:, :], ALU.mult).then_inc(norm_step, 1)
                    wait_apart(pool, norm_step, 3 * b + 3)
                    nc.gpsimd.tensor_scalar(nshift[:, :], nshift[:, :], -1.0, None, ALU.mult).then_inc(norm_ready, 1)
                    if not first:
                        scatter(b - 1, 1 - u)

                batches(pool, body)
                scatter(NB - 1, 1)
                for u in range(2):
                    pool.wait_ge(entries_written[u], 16 * 2 * TILES * (NB // 2))

            @block_a.scalar
            def _(act):
                def split_xt_hi(b, pair, u, first):
                    act.wait_ge(xt_loaded[u], 16 * (pair + 1))
                    if not first:
                        act.wait_ge(q_ready, PAIRS * b)
                        act.wait_ge(xt_lo_done, b)
                    nc.scalar.activation(xt_hi[:, :], xt_raw[u][:, :], ACT.Copy).then_inc(xt_hi_done, 1)

                def split_x_hi(b, pair, u, first):
                    act.wait_ge(x_loaded[u], 16 * (pair + 1))
                    if not first:
                        act.wait_ge(kt_used, PAIRS * b)
                        act.wait_ge(x_lo_done, b)
                    nc.scalar.activation(x_hi[:, :, :], x_raw[u][:, :, :], ACT.Copy).then_inc(x_hi_done, 1)

                def evacuate_x1t(j, b_prev):
                    act.wait_ge(x1t_ready, PAIRS * b_prev + j + 1)
                    if j >= 2:
                        act.wait_ge(logits_ready, PAIRS * b_prev + j - 1)
                    nc.scalar.activation(x1t[:, j % 2, :], t_ps[:, j % 2, :], ACT.Copy).then_inc(x1t_done, 1)

                def route_exp(b_prev):
                    act.wait_ge(gap_ready, b_prev + 1)
                    nc.scalar.activation(gap_exp[:, :], gap[:, :], ACT.Exp).then_inc(gap_exp_done, 1)

                split_xt_hi(0, 0, 0, True)
                split_x_hi(0, 0, 0, True)

                def body(pair, u, first, last):
                    b = pair * 2 + u
                    nxt = pair if u == 0 else pair + 1
                    if not first:
                        act.wait_ge(kt_ready, PAIRS * b)
                        act.wait_ge(qt_ready, PAIRS * b)
                    for o in range(DK):
                        act.wait_ge(k_max_done, DK * b + o + 1)
                        nc.scalar.activation(k_exp[:, o, :], k_ps[:, o, :], ACT.Exp, bias=nk_max[:, u, o:o + 1],
                                             accum_out=zk[:, u, o:o + 1]).then_inc(k_exp_done, 1)
                    for t in range(TILES):
                        if t % 2 == 0:
                            act.wait_ge(q_max_done, PAIRS * b + t // 2 + 1)
                        h = (t // 2) % 2
                        nc.scalar.activation(q_exp[:, t, :], qo_ps[:, h, (t % 2) * D:(t % 2 + 1) * D], ACT.Exp,
                                             bias=nq_max[:, u, t:t + 1], accum_out=zq[:, u, t:t + 1]).then_inc(q_exp_done, 1)
                    for j in range(PAIRS):
                        act.wait_ge(kt_ready, PAIRS * b + j + 1)
                        if j < 2:
                            if not first:
                                act.wait_ge(kt_used, PAIRS * b + j - 1)
                        else:
                            act.wait_ge(kt_used, PAIRS * b + j - 1)
                        nc.scalar.activation(kt_hi[:, j % 2, :], t_ps[:, j % 2, :], ACT.Copy).then_inc(kt_hi_done, 1)
                        if j == 1 and not last:
                            split_xt_hi(b + 1, nxt, 1 - u, False)
                    act.wait_ge(kt_used, PAIRS * (b + 1))
                    if not first:
                        act.wait_ge(m_ready, b)
                    nc.scalar.activation(g_hi[:, :, :], g_ps, ACT.Copy).then_inc(g_hi_done, 1)

                    def qt(j):
                        act.wait_ge(qt_ready, PAIRS * b + j + 1)
                        if j >= 2 or not first:
                            act.wait_ge(o_ready, PAIRS * b + j - 1)
                        nc.scalar.activation(qt_hi[:, j % 2, :], t_ps[:, j % 2, :], ACT.Copy).then_inc(qt_hi_done, 1)

                    qt(0)
                    qt(1)
                    if not first:
                        for j in range(PAIRS):
                            evacuate_x1t(j, b - 1)
                    qt(2)
                    qt(3)
                    if not last:
                        split_x_hi(b + 1, nxt, 1 - u, False)
                    if not first:
                        route_exp(b - 1)
                    act.wait_ge(norm_ready, b + 1)
                    if not (isinstance(pair, int) and pair == 0):
                        act.wait_ge(x1_stored[u], 32 * pair)
                    for t in range(TILES):
                        ins = nc.scalar.activation(x1_sb[u][:, t, :], r_sb[:, t, :], ACT.Identity,
                                                   bias=nshift[:, t:t + 1], scale=rstd[:, t:t + 1])
                    ins.then_inc(x1_done, 1)

                batches(act, body)
                for j in range(PAIRS):
                    evacuate_x1t(j, NB - 1)
                route_exp(NB - 1)

            @block_a.vector
            def _(dve):
                dve.wait_ge(consts_loaded, 96)
                dve.wait_ge(consts_made, 1)
                for i, hi in enumerate((wk_hi, wq_hi)):
                    nc.vector.tensor_copy(hi[:, :, :].rearrange("p k d -> p (k d)"), w_in[:, i, :]).then_inc(consts_split, 1)
                for src, dst in ((ident, ident_r), (tri_f, tri_r), (ones_f, ones_r)):
                    nc.vector.tensor_copy(dst[:, :], src[:, :]).then_inc(consts_split, 1)
                dve.wait_ge(consts_split, 5)
                for i, (hi, lo) in enumerate(((wk_hi, wk_lo), (wq_hi, wq_lo))):
                    nc.vector.tensor_tensor(lo[:, :, :].rearrange("p k d -> p (k d)"), w_in[:, i, :],
                                            hi[:, :, :].rearrange("p k d -> p (k d)").bitcast(F),
                                            ALU.subtract).then_inc(consts_split, 1)

                def split_xt_lo(b, u, first):
                    dve.wait_ge(xt_hi_done, b + 1)
                    if not first:
                        dve.wait_ge(q_ready, PAIRS * b)
                    nc.vector.tensor_tensor(xt_lo[:, :], xt_raw[u][:, :], xt_hi[:, :].bitcast(F),
                                            ALU.subtract).then_inc(xt_lo_done, 1)

                split_xt_lo(0, 0, True)
                dve.wait_ge(wvo_ready, 1)
                wvo = t_ps[:, 0, :].rearrange("p (k d) -> p k d", k=DK)
                nc.vector.tensor_copy(wvo_hi[:, :, :], wvo).then_inc(consts_split, 1)
                dve.wait_ge(consts_split, 8)
                nc.vector.tensor_tensor(wvo_lo[:, :, :], wvo, wvo_hi[:, :, :].bitcast(F), ALU.subtract).then_inc(consts_split, 1)

                ROUTE_STEPS = 30

                def route(b, pair, u, part, state={}):
                    def step(ins):
                        ins.then_inc(route_step, 1)
                        state["k"] += 1
                        dve.wait_ge(route_step, ROUTE_STEPS * b + state["k"])

                    V = nc.vector
                    over_tiles = lambda a: a.rearrange("p (a e) -> p a e", a=1).broadcast_to([P, TILES, E])
                    over_experts = lambda a: a.rearrange("p (t a) -> p t a", a=1).broadcast_to([P, TILES, E])
                    if part == 0:
                        state["k"] = 0
                        dve.wait_ge(logits_ready, PAIRS * (b + 1))
                        step(V.tensor_copy(logits[:, :, :], l_ps))
                        for c, src in enumerate((logits, second)):
                            if c == 1:
                                step(V.scalar_tensor_tensor(second[:, :, :], pick[0][:, :, :], -3.0e38, logits[:, :, :],
                                                            ALU.mult, ALU.add))
                            step(V.reduce_max(top[:, c, :], src[:, :, :], X))
                            step(V.tensor_tensor(eq[:, :, :], src[:, :, :], over_experts(top[:, c, :]), ALU.is_equal))
                            step(V.tensor_tensor(score[:, :, :], eq[:, :, :], over_tiles(order_w[:, :]), ALU.mult))
                            step(V.reduce_max(best[:, :], score[:, :, :], X))
                            step(V.tensor_tensor(pick[c][:, :, :], score[:, :, :], over_experts(best[:, :]), ALU.is_equal))
                        step(V.tensor_tensor(mask[:, :, :], pick[0][:, :, :], pick[1][:, :, :], ALU.add))
                        V.tensor_tensor(gap[:, :], top[:, 1, :], top[:, 0, :], ALU.subtract).then_inc(gap_ready, 1)
                        step(V.tensor_reduce(mask_sum_f[:, :], mask[:, :, :].bitcast(F).rearrange("p t e -> p e t"), X, ALU.add))
                        V.tensor_copy(mask_sum[:, :], mask_sum_f[:, :]).then_inc(mask_ready, 1)
                    else:
                        dve.wait_ge(gap_exp_done, b + 1)
                        step(V.tensor_scalar(gate_sum[:, :], gap_exp[:, :], 1.0, None, ALU.add))
                        step(V.reciprocal(gates[:, 0, :], gate_sum[:, :]))
                        step(V.tensor_tensor(gates[:, 1, :], gap_exp[:, :], gates[:, 0, :], ALU.mult))
                        dve.wait_ge(rank_ready, b + 1)
                        step(V.tensor_tensor(slot[:, :, :], rank_ps, over_tiles(rank_base[:, :]), ALU.add))
                        step(V.tensor_scalar(late[:, :, :], slot[:, :, :], float(CAP), DROPPED, ALU.is_ge, ALU.mult))
                        step(V.tensor_tensor(slot[:, :, :], slot[:, :, :], over_tiles(slot_base[:, :]), ALU.add))
                        step(V.tensor_tensor(slot[:, :, :], slot[:, :, :], late[:, :, :], ALU.add))
                        step(V.tensor_tensor(rank_base[:, :], rank_base[:, :], total_ps, ALU.add))
                        for c in range(2):
                            step(V.tensor_tensor(pick[c][:, :, :], pick[c][:, :, :], slot[:, :, :], ALU.mult))
                            step(V.tensor_reduce(slot_f[:, c, :], pick[c][:, :, :], X, ALU.add))
                        step(V.tensor_copy(slot_i[:, :, :], slot_f[:, :, :]))
                        step(V.tensor_scalar(slot_p[:, :, :], slot_i[:, :, :], P - 1, None, ALU.bitwise_and))
                        step(V.tensor_scalar(slot_c[:, :, :], slot_i[:, :, :], P.bit_length() - 1, None,
                                             ALU.arith_shift_right))
                        if not (isinstance(pair, int) and pair == 0):
                            dve.wait_ge(entries_written[u], 16 * 2 * TILES * pair)
                        for c in range(2):
                            V.tensor_copy(entry[u][:, c, :, 0], token_id[:, :])
                        V.tensor_copy(entry[u][:, :, :, 1].bitcast(F), gates[:, :, :])
                        V.scalar_tensor_tensor(where[u][:, :, :], slot_p[:, :, :], float(TCOLS), slot_c[:, :, :],
                                               ALU.mult, ALU.add).then_inc(slots_ready, 1)
                        dve.wait_ge(slots_ready, b + 1)
                        V.tensor_scalar(token_id[:, :], token_id[:, :], N, None, ALU.add).then_inc(route_step, 1)
                        state["k"] += 1
                        dve.wait_ge(route_step, ROUTE_STEPS * b + state["k"])
                        assert state["k"] == ROUTE_STEPS, state["k"]

                def body(pair, u, first, last):
                    b = pair * 2 + u
                    V = nc.vector
                    for o in range(DK):
                        dve.wait_ge(k_ready, DK * b + o + 1)
                        V.reduce_max(nk_max[:, u, o:o + 1], k_ps[:, o, :], X, negate=True).then_inc(k_max_done, 1)
                    for j in range(PAIRS):
                        dve.wait_ge(q_ready, PAIRS * b + j + 1)
                        V.reduce_max(nq_max[:, u, 2 * j:2 * j + 2], qo_ps[:, j % 2, :].rearrange("p (t d) -> p t d", t=2), X,
                                     negate=True).then_inc(q_max_done, 1)

                    def kt(j):
                        dve.wait_ge(kt_hi_done, PAIRS * b + j + 1)
                        V.tensor_tensor(kt_lo[:, j % 2, :], t_ps[:, j % 2, :], kt_hi[:, j % 2, :].bitcast(F),
                                        ALU.subtract).then_inc(kt_lo_done, 1)

                    kt(0)
                    kt(1)
                    dve.wait_ge(k_exp_done, DK * (b + 1))
                    dve.wait_ge(q_exp_done, TILES * (b + 1))
                    V.reciprocal(rzk[:, :], zk[:, u, :]).then_inc(z_done, 1)
                    V.reciprocal(rzq[:, :], zq[:, u, :]).then_inc(z_done, 1)
                    dve.wait_ge(z_done, 3 * b + 2)
                    V.tensor_scalar(rzk[:, :], rzk[:, :], CTX_SCALE, None, ALU.mult).then_inc(z_done, 1)
                    kt(2)
                    kt(3)
                    dve.wait_ge(g_hi_done, b + 1)
                    V.tensor_tensor(g_lo[:, :, :], g_ps, g_hi[:, :, :].bitcast(F), ALU.subtract).then_inc(g_lo_done, 1)

                    def qt(j):
                        dve.wait_ge(qt_hi_done, PAIRS * b + j + 1)
                        V.tensor_tensor(qt_lo[:, j % 2, :], t_ps[:, j % 2, :], qt_hi[:, j % 2, :].bitcast(F),
                                        ALU.subtract).then_inc(qt_lo_done, 1)

                    qt(0)
                    qt(1)
                    if not last:
                        split_xt_lo(b + 1, 1 - u, False)
                    dve.wait_ge(m_ready, b + 1)
                    dve.wait_ge(z_done, 3 * b + 3)
                    for o in range(DK):
                        V.scalar_tensor_tensor(m_raw[:, o, :], m_ps[:, o, :], rzk[:, o:o + 1], bo_sb[:, :],
                                               ALU.mult, ALU.add).then_inc(m_raw_done, 1)
                    dve.wait_ge(m_raw_done, DK * (b + 1))
                    V.tensor_copy(m_hi[:, :, :], m_raw[:, :, :]).then_inc(m_hi_done, 1)
                    dve.wait_ge(m_hi_done, b + 1)
                    V.tensor_tensor(m_lo[:, :, :], m_raw[:, :, :], m_hi[:, :, :].bitcast(F), ALU.subtract).then_inc(m_lo_done, 1)

                    def residual(j):
                        dve.wait_ge(o_ready, PAIRS * b + j + 1)
                        if j == 0 and not first:
                            dve.wait_ge(x1_done, b)
                        for t in (2 * j, 2 * j + 1):
                            V.scalar_tensor_tensor(r_sb[:, t, :], qo_ps[:, j % 2, (t % 2) * D:(t % 2 + 1) * D],
                                                   rzq[:, t:t + 1], x_raw[u][:, t, :], ALU.mult, ALU.add).then_inc(r_done, 1)
                        for t in (2 * j, 2 * j + 1):
                            dve.wait_ge(r_done, TILES * b + t + 1)
                            V.bn_stats(stats[:, t, :], r_sb[:, t, :]).then_inc(stats_done, 1)

                    qt(2)
                    residual(0)
                    qt(3)
                    if not first:
                        route(b - 1, None if u == 0 else pair, 1 - u, 0)
                    for j in range(1, PAIRS):
                        residual(j)
                    if not first:
                        dve.wait_ge(norm_ready, b)
                    wait_apart(dve, stats_done, TILES * (b + 1))
                    for t in range(TILES):
                        ins = V.bn_aggr(mean_var[:, t, :], stats[:, t, :])
                    ins.then_inc(mean_done, 1)
                    if not first:
                        prev = pair if u == 1 else pair - 1
                        route(b - 1, prev, 1 - u, 1)

                batches(dve, body, peeled=2)
                route(NB - 1, NB // 2 - 1, 1, 0)
                route(NB - 1, NB // 2 - 1, 1, 1)
                dve.wait_ge(w_loaded, 32)
                nc.vector.tensor_copy(w_hi[0][:, :], w_raw[:, :]).then_inc(w_split, 1)
                dve.wait_ge(w_split, 1)
                nc.vector.tensor_tensor(w_lo[0][:, :], w_raw[:, :], w_hi[0][:, :].bitcast(F), ALU.subtract).then_inc(w_split, 1)
                dve.wait_ge(w_split, 2)

            @block_a.tensor
            def _(pe):
                def product(dst, a, b, start, stop):
                    nc.tensor.matmul(dst, a[0], b[0], start=start, stop=False)
                    nc.tensor.matmul(dst, a[0], b[1], start=False, stop=False)
                    return nc.tensor.matmul(dst, a[1], b[0], start=False, stop=stop)

                pe.wait_ge(consts_loaded, 96)
                wv_in = w_in[:, 2, :].rearrange("p (k d) -> p k d", k=DK)
                wo_in = w_in[:, 3, :].rearrange("p (k d) -> p k d", k=DK)
                for i in range(DK):
                    for o in range(DK):
                        ins = nc.tensor.matmul(t_ps[:, 0, i * D:(i + 1) * D], wv_in[:, o, i * P:(i + 1) * P], wo_in[:, o, :],
                                               start=(o == 0), stop=(o == DK - 1))
                ins.then_inc(wvo_ready, 1)
                pe.wait_ge(consts_split, 7)

                xt = [a[:, :].rearrange("p (k t n) -> p k t n", k=DK, t=TILES) for a in (xt_hi, xt_lo)]

                def transpose_x1(j, b_prev, u_prev):
                    pe.wait_ge(x1_done, b_prev + 1)
                    if j >= 2:
                        pe.wait_ge(x1t_done, PAIRS * b_prev + j - 1)
                    for i in range(2):
                        for k in range(DK):
                            c = (i * DK + k) * P
                            ins = nc.tensor.transpose(t_ps[:, j % 2, c:c + P], x1_sb[u_prev][:, 2 * j + i, k * P:(k + 1) * P], ident[:, :])
                    ins.then_inc(x1t_ready, 1)

                def router(j, b_prev):
                    pe.wait_ge(x1t_done, PAIRS * b_prev + j + 1)
                    for i in range(2):
                        for k in range(DK):
                            c = (i * DK + k) * P
                            ins = nc.tensor.matmul(l_ps[:, 2 * j + i, :], x1t[:, j % 2, c:c + P], wr_sb[:, k, :],
                                                   start=(k == 0), stop=(k == DK - 1))
                    ins.then_inc(logits_ready, 1)

                def rank(b_prev):
                    pe.wait_ge(mask_ready, b_prev + 1)
                    nc.tensor.matmul(total_ps, ones_r[:, :], mask_sum[:, :], start=True, stop=True)
                    nc.tensor.matmul(rank_ps, tri_r[:, :], mask_sum[:, :].rearrange("p (a e) -> p a e", a=1).broadcast_to([P, TILES, E]),
                                     start=True, stop=False)
                    for t in range(TILES - 1):
                        ins = nc.tensor.matmul(rank_ps[:, t + 1:TILES, :], ident_r[:, :],
                                               mask[:, t:t + 1, :].broadcast_to([P, TILES - 1 - t, E]),
                                               start=False, stop=(t == TILES - 2))
                    ins.then_inc(rank_ready, 1)

                def body(pair, u, first, last):
                    b = pair * 2 + u
                    pe.wait_ge(xt_lo_done, b + 1)
                    if not first:
                        pe.wait_ge(m_raw_done, DK * b)
                    for o in range(DK):
                        if o == 1 and not (isinstance(pair, int) and pair == 0):
                            pe.wait_ge(slots_ready, b - 1)
                        for i in range(3 * DK):
                            k, part = i // 3, i % 3
                            w = (wk_hi, wk_hi, wk_lo)[part]
                            v = (xt_hi, xt_lo, xt_hi)[part]
                            for h in range(2):
                                ins = nc.tensor.matmul(k_ps[:, o, h * 512:(h + 1) * 512], w[:, k, o * P:(o + 1) * P],
                                                       v[:, k * N + h * 512:k * N + (h + 1) * 512], start=(i == 0), stop=(i == 3 * DK - 1))
                        ins.then_inc(k_ready, 1)
                    for j in range(PAIRS):
                        if j >= 2:
                            pe.wait_ge(q_exp_done, TILES * b + 2 * (j - 1))
                        elif not first:
                            pe.wait_ge(r_done, TILES * (b - 1) + 2 * (j + 3))
                        for i in range(2):
                            for k in range(DK):
                                t = 2 * j + i
                                ins = product(qo_ps[:, j % 2, i * D:(i + 1) * D],
                                              (xt[0][:, k, t, :], xt[1][:, k, t, :]), (wq_hi[:, k, :], wq_lo[:, k, :]),
                                              k == 0, k == DK - 1)
                        ins.then_inc(q_ready, 1)

                    def transpose_k(j):
                        if j == 0:
                            pe.wait_ge(k_exp_done, DK * (b + 1))
                        if j >= 2:
                            pe.wait_ge(kt_lo_done, PAIRS * b + j - 1)
                        elif not first:
                            pe.wait_ge(qt_lo_done, PAIRS * (b - 1) + j + 3)
                        for i in range(2):
                            t = 2 * j + i
                            for o in range(DK):
                                c = i * D + o * P
                                ins = nc.tensor.transpose(t_ps[:, j % 2, c:c + P], k_exp[:, o, t * P:(t + 1) * P], ident[:, :])
                        ins.then_inc(kt_ready, 1)

                    def context(j):
                        pe.wait_ge(kt_lo_done, PAIRS * b + j + 1)
                        if j == 0:
                            pe.wait_ge(x_lo_done, b + 1)
                        for i in range(2):
                            t = 2 * j + i
                            for k in range(DK):
                                c = i * D
                                ins = product(g_ps[:, k, :], (x_hi[:, t, k * P:(k + 1) * P], x_lo[:, t, k * P:(k + 1) * P]),
                                              (kt_hi[:, j % 2, c:c + D], kt_lo[:, j % 2, c:c + D]), t == 0, t == TILES - 1)
                        ins.then_inc(kt_used, 1)

                    def transpose_q(j):
                        if j == 0:
                            pe.wait_ge(q_exp_done, TILES * (b + 1))
                        if j < 2:
                            pe.wait_ge(kt_lo_done, PAIRS * b + j + 3)
                        elif first:
                            pe.wait_ge(qt_lo_done, PAIRS * b + j - 1)
                        else:
                            pe.wait_ge(x1t_done, PAIRS * (b - 1) + j + 1)
                        for i in range(2):
                            t = 2 * j + i
                            for o in range(DK):
                                c = i * D + o * P
                                ins = nc.tensor.transpose(t_ps[:, j % 2, c:c + P], q_exp[:, t, o * P:(o + 1) * P], ident[:, :])
                        ins.then_inc(qt_ready, 1)

                    def attend(j):
                        pe.wait_ge(qt_lo_done, PAIRS * b + j + 1)
                        if j == 0:
                            pe.wait_ge(m_lo_done, b + 1)
                        if j < 2:
                            pe.wait_ge(q_exp_done, TILES * b + 2 * (j + 3))
                        else:
                            pe.wait_ge(r_done, TILES * b + 2 * (j - 1))
                        for i in range(2):
                            for o in range(DK):
                                c = i * D + o * P
                                ins = product(qo_ps[:, j % 2, i * D:(i + 1) * D],
                                              (qt_hi[:, j % 2, c:c + P], qt_lo[:, j % 2, c:c + P]), (m_hi[:, o, :], m_lo[:, o, :]),
                                              o == 0, o == DK - 1)
                        ins.then_inc(o_ready, 1)

                    transpose_k(0)
                    transpose_k(1)
                    context(0)
                    transpose_k(2)
                    context(1)
                    transpose_k(3)
                    context(2)
                    context(3)
                    transpose_q(0)
                    transpose_q(1)
                    if not first:
                        pe.wait_ge(qt_lo_done, PAIRS * b + 1)
                        transpose_x1(0, b - 1, 1 - u)
                        pe.wait_ge(qt_lo_done, PAIRS * b + 2)
                        transpose_x1(1, b - 1, 1 - u)
                    pe.wait_ge(g_lo_done, b + 1)
                    if first:
                        pe.wait_ge(consts_split, 9)
                    for o in range(DK):
                        for i in range(DK):
                            ins = product(m_ps[:, o, :], (g_hi[:, i, o * P:(o + 1) * P], g_lo[:, i, o * P:(o + 1) * P]),
                                          (wvo_hi[:, i, :], wvo_lo[:, i, :]), i == 0, i == DK - 1)
                    ins.then_inc(m_ready, 1)
                    if not first:
                        router(0, b - 1)
                        transpose_x1(2, b - 1, 1 - u)
                        router(1, b - 1)
                        transpose_x1(3, b - 1, 1 - u)
                        router(2, b - 1)
                        router(3, b - 1)
                    transpose_q(2)
                    attend(0)
                    transpose_q(3)
                    attend(1)
                    attend(2)
                    attend(3)
                    if not first:
                        rank(b - 1)

                batches(pe, body)
                b = NB - 1
                for j in range(2):
                    pe.wait_ge(qt_lo_done, PAIRS * b + j + 3)
                    transpose_x1(j, b, 1)
                pe.wait_ge(slots_ready, b)
                for j in range(PAIRS):
                    router(j, b)
                    if j < 2:
                        transpose_x1(j + 2, b, 1)
                rank(b)

        with ExitStack() as phase:
            def sb(name, shape, dt=F):
                return phase.enter_context(nc.sbuf_tensor(name, shape, dt))

            def ps(name, shape):
                return phase.enter_context(nc.psum_tensor(name, shape, F))

            w_hi[1] = sb("w_hi1", [P, 2 * DK * FF], R)
            w_lo[1] = sb("w_lo1", [P, 2 * DK * FF], R)
            table = sb("table", [P, BT + TCOLS + 2 * BT, 2], I)
            pick_idx = [sb(f"pick_idx{i}", [P, BT], I) for i in range(2)]
            put_idx = sb("put_idx", [P, BT], I)
            put_gate = sb("put_gate", [P, BT])
            rows = [sb(f"rows{i}", [P, BT, D]) for i in range(2)]
            xt_hi = [sb(f"bt_hi{i}", [P, DK, BLK], R) for i in range(2)]
            xt_lo = [sb(f"bt_lo{i}", [P, DK, BLK], R) for i in range(2)]
            h_hi = sb("h_hi", [P, 4, BLK], R)
            h_lo = sb("h_lo", [P, 4, BLK], R)
            yt = sb("yt", [P, DK, BLK])
            y = sb("y", [P, BT, D])

            h_ps = ps("h_ps", [P, 4, BLK])
            y_ps = ps("y_ps", [P, DK, BLK])
            t_ps = ps("tb_ps", [P, 2 * BLK])

            table_loaded, table_padded = sem("table_loaded"), sem("table_padded")
            idx_ready, gathered = sems("idx_ready", 2), sems("gathered", 2)
            put_ready, added = sem("put_ready"), sem("added")
            xt_ready, bt_hi_done, bt_lo_done = sem("xt_ready"), sem("bt_hi_done"), sem("bt_lo_done")
            h_ready, gelu_done, h_hi_done, h_lo_done, h_used = (
                sem("h_ready"), sem("gelu_done"), sem("h_hi_done"), sem("h_lo_done"), sem("h_used"))
            yt_done, y_ready, y_done = sem("yt_done"), sem("y_ready"), sem("y_done")

            block_b = phase.enter_context(nc.Block())

            def experts(eng, body, between=None):
                with eng.Fori(0, E // 2) as half:
                    for eu in range(2):
                        if between is not None:
                            between(half, eu)
                        with eng.Fori(0, BLOCKS // 2) as bp:
                            for bu in range(2):
                                n = (half * 2 + eu) * BLOCKS + bp * 2 + bu
                                body(n, half * 2 + eu, eu, bu, bp)

            @block_b.sync
            def _(sp):
                sp.dma_start(table[:, BT:BT + TCOLS, :].rearrange("p c w -> p (c w)"), table_rows).then_inc(table_loaded, 16)
                with sp.Fori(0, E - 1) as e:
                    sp.wait_ge(w_split, 2 + 8 * 2 * e)
                    load_expert(sp, e + 1)

            @block_b.gpsimd
            def _(pool):
                G = nc.gpsimd
                G.memset(table[:, 0:BT, :], 0).then_inc(table_padded, 1)
                G.memset(table[:, BT + TCOLS:, :], 0).then_inc(table_padded, 1)
                pool.wait_ge(table_padded, 2)
                G.iota(table[:, 0:BT, 0], pattern=[[P, BT]], base=T, channel_multiplier=1).then_inc(table_padded, 1)
                G.iota(table[:, BT + TCOLS:, 0].rearrange("p (a t) -> p a t", t=BT), pattern=[[0, 2], [P, BT]], base=T, channel_multiplier=1).then_inc(table_padded, 1)
                pool.wait_ge(table_padded, 4)
                pool.wait_ge(table_loaded, 16)

                def gather(n, u, uses):
                    G.tensor_copy(pick_idx[u][:, :], table[:, bass.ds(n * BT + BT, BT), 0]).then_inc(idx_ready[u], 1)
                    wait_apart(pool, idx_ready[u], uses + 1)
                    for t in range(BT):
                        pool.indirect_dma_start(
                            out=rows[u][:, t, :], out_offset=None, in_=x1_dram,
                            in_offset=bass.IndirectOffsetOnAxis(ap=pick_idx[u][:, t:t + 1], axis=0)).then_inc(gathered[u], 16)

                def put(n):
                    G.tensor_copy(put_idx[:, :], table[:, bass.ds(n * BT, BT), 0])
                    G.tensor_copy(put_gate[:, :], table[:, bass.ds(n * BT, BT), 1].bitcast(F)).then_inc(put_ready, 1)
                    pool.wait_ge(y_done, n + 1)
                    wait_apart(pool, put_ready, n + 1)
                    for t in range(BT):
                        pool.indirect_dma_start(
                            out=acc_dram, out_offset=bass.IndirectOffsetOnAxis(ap=put_idx[:, t:t + 1], axis=0),
                            in_=y[:, t, :], in_offset=None, compute_op=ALU.add).then_inc(added, 16)
                    pool.wait_ge(added, 16 * BT * (n + 1))

                gather(0, 0, 0)
                gather(1, 1, 0)

                def body(n, e, eu, bu, bp):
                    pool.wait_ge(xt_ready, n + 1)
                    gather(n + 2, bu, e * (BLOCKS // 2) + bp + 1)
                    put(n)

                experts(pool, body)
                put(E * BLOCKS)
                for u in range(2):
                    pool.wait_ge(gathered[u], 16 * BT * (E * BLOCKS // 2 + 1))

            @block_b.scalar
            def _(act):
                def split_hi(n, u):
                    act.wait_ge(xt_ready, n + 1)
                    nc.scalar.activation(xt_hi[u][:, :, :].rearrange("p k n -> p (k n)"), t_ps[:, :], ACT.Copy).then_inc(bt_hi_done, 1)

                split_hi(0, 0)

                def body(n, e, eu, bu, bp):
                    for f in range(FT):
                        c = f % 4
                        wait_apart(act, h_ready, n * FT + f + 1)
                        nc.scalar.activation(h_ps[:, c, :], h_ps[:, c, :], ACT.Gelu_apprx_tanh,
                                             bias=b1_sb[:, bass.ds(e * FT + f, 1)]).then_inc(gelu_done, 1)
                        act.wait_ge(gelu_done, n * FT + f + 1)
                        if f >= 4:
                            act.wait_ge(h_used, n * FT + f - 3)
                        nc.scalar.activation(h_hi[:, c, :], h_ps[:, c, :], ACT.Copy).then_inc(h_hi_done, 1)
                        if f == 5:
                            split_hi(n + 1, 1 - bu)
                    act.wait_ge(h_used, (n + 1) * FT)
                    wait_apart(act, y_ready, n + 1)
                    for k in range(DK):
                        ins = nc.scalar.activation(yt[:, k, :], y_ps[:, k, :], ACT.Identity,
                                                   bias=b2_sb[:, bass.ds(e * DK + k, 1)])
                    ins.then_inc(yt_done, 1)

                experts(act, body)

            @block_b.vector
            def _(dve):
                V = nc.vector
                V.memset(yt[:, :, :], 0.0).then_inc(yt_done, 1)

                def split_lo(n, u):
                    dve.wait_ge(bt_hi_done, n + 1)
                    V.tensor_tensor(xt_lo[u][:, :, :].rearrange("p k n -> p (k n)"), t_ps[:, :],
                                    xt_hi[u][:, :, :].rearrange("p k n -> p (k n)").bitcast(F), ALU.subtract).then_inc(bt_lo_done, 1)

                def scale_y(n):
                    dve.wait_ge(y_ready, n + 1)
                    dve.wait_ge(put_ready, n + 1)
                    for t in range(BT):
                        ins = V.tensor_scalar(y[:, t, :], t_ps[:, t * D:(t + 1) * D], put_gate[:, t:t + 1], None, ALU.mult)
                    ins.then_inc(y_done, 1)

                split_lo(0, 0)

                def body(n, e, eu, bu, bp, weights=None):
                    for f in range(FT):
                        c = f % 4
                        dve.wait_ge(h_hi_done, n * FT + f + 1)
                        V.tensor_tensor(h_lo[:, c, :], h_ps[:, c, :], h_hi[:, c, :].bitcast(F), ALU.subtract).then_inc(h_lo_done, 1)
                        if f == 2 and weights is not None:
                            weights()
                        if f == 3:
                            scale_y(n)
                        if f == 5:
                            split_lo(n + 1, 1 - bu)

                CH = 2 * DK * FF // 8

                def expert(half, eu, last):
                    e = half * 2 + eu
                    other = 1 - eu
                    with dve.Fori(0, 4) as bp:
                        for bu in range(2):
                            piece = bp * 2 + bu

                            def split_weights():
                                c0 = piece * CH
                                dve.wait_ge(w_loaded, 32 * (e + 2))
                                V.tensor_copy(w_hi[other][:, bass.ds(c0, CH)], w_raw[:, bass.ds(c0, CH)]).then_inc(w_split, 1)
                                dve.wait_ge(w_split, 3 + e * 16 + piece * 2)
                                V.tensor_tensor(w_lo[other][:, bass.ds(c0, CH)], w_raw[:, bass.ds(c0, CH)],
                                                w_hi[other][:, bass.ds(c0, CH)].bitcast(F), ALU.subtract).then_inc(w_split, 1)

                            body(e * BLOCKS + piece, e, eu, bu, bp, None if last else split_weights)
                    for bu in range(2):
                        body(e * BLOCKS + 8 + bu, e, eu, bu, 4)

                with dve.Fori(0, E // 2 - 1) as half:
                    for eu in range(2):
                        expert(half, eu, False)
                expert(E // 2 - 1, 0, False)
                expert(E // 2 - 1, 1, True)
                scale_y(E * BLOCKS)

            @block_b.tensor
            def _(pe):
                def transpose_rows(n, u, uses):
                    pe.wait_ge(gathered[u], 16 * BT * (uses + 1))
                    pe.wait_ge(y_done, n)
                    for k in range(DK):
                        for t in range(BT):
                            c = k * BLK + t * P
                            ins = nc.tensor.transpose(t_ps[:, c:c + P], rows[u][:, t, k * P:(k + 1) * P], ident[:, :])
                    ins.then_inc(xt_ready, 1)

                def transpose_y(n):
                    pe.wait_ge(bt_lo_done, n + 1)
                    for t in range(BT):
                        for k in range(DK):
                            c = t * D + k * P
                            ins = nc.tensor.transpose(t_ps[:, c:c + P], yt[:, k, t * P:(t + 1) * P], ident[:, :])
                    ins.then_inc(y_ready, 1)

                pe.wait_ge(gathered[0], 16 * BT)
                for k in range(DK):
                    for t in range(BT):
                        c = k * BLK + t * P
                        ins = nc.tensor.transpose(t_ps[:, c:c + P], rows[0][:, t, k * P:(k + 1) * P], ident[:, :])
                ins.then_inc(xt_ready, 1)

                def between(half, eu):
                    wait_apart(pe, w_split, 2 + 16 * (half * 2 + eu))

                def body(n, e, eu, bu, bp):
                    def up(f):
                        if f == 0:
                            pe.wait_ge(bt_lo_done, n + 1)
                        for i in range(3 * DK):
                            k, part = i // 3, i % 3
                            w = (w_hi, w_hi, w_lo)[part][eu]
                            v = (xt_hi, xt_lo, xt_hi)[part][bu]
                            c = k * FF + f * P
                            ins = nc.tensor.matmul(h_ps[:, f % 4, :], w[:, c:c + P], v[:, k, :], start=(i == 0), stop=(i == 3 * DK - 1))
                        ins.then_inc(h_ready, 1)

                    def down(f):
                        pe.wait_ge(h_lo_done, n * FT + f + 1)
                        if f == 0:
                            pe.wait_ge(yt_done, n + 1)
                        for k in range(DK):
                            for part in range(3):
                                w = (w_hi, w_hi, w_lo)[part][eu]
                                v = (h_hi, h_lo, h_hi)[part]
                                c = W1 + f * D + k * P
                                ins = nc.tensor.matmul(y_ps[:, k, :], w[:, c:c + P], v[:, f % 4, :],
                                                       start=(f == 0 and part == 0), stop=(f == FT - 1 and part == 2))
                        ins.then_inc(h_used, 1)

                    up(0)
                    up(1)
                    up(2)
                    down(0)
                    up(3)
                    down(1)
                    transpose_y(n)
                    up(4)
                    down(2)
                    transpose_rows(n + 1, 1 - bu, e * (BLOCKS // 2) + bp + bu)
                    up(5)
                    down(3)
                    up(6)
                    down(4)
                    up(7)
                    down(5)
                    down(6)
                    down(7)

                experts(pe, body, between)
                pe.wait_ge(yt_done, E * BLOCKS + 1)
                transpose_y(E * BLOCKS)

        with ExitStack() as phase:
            RING = 4
            s_in = [phase.enter_context(nc.sbuf_tensor(f"s_in{i}", [P, TILES, D], F)) for i in range(RING)]
            s_out = [phase.enter_context(nc.sbuf_tensor(f"s_out{i}", [P, TILES, D], F)) for i in range(RING)]
            stats = phase.enter_context(nc.sbuf_tensor("stats_c", [P, RING, TILES, 6], F))
            mean_var = phase.enter_context(nc.sbuf_tensor("mean_var_c", [P, RING, TILES, 2], F))
            rstd = phase.enter_context(nc.sbuf_tensor("rstd_c", [P, RING, TILES], F))
            nshift = phase.enter_context(nc.sbuf_tensor("nshift_c", [P, RING, TILES], F))
            minus_half = phase.enter_context(nc.sbuf_tensor("minus_half_c", [P, TILES], F))
            s_loaded, s_stored = sems("s_loaded", RING), sems("s_stored", RING)
            half_made, stats_done, mean_done = sem("half_made"), sem("stats_done_c"), sem("mean_done_c")
            norm_step, norm_ready, s_done = sem("norm_step_c"), sem("norm_ready_c"), sem("s_done")

            block_c = phase.enter_context(nc.Block())

            @block_c.sync
            def _(sp):
                def load(b, r):
                    sp.dma_start(s_in[r][:, :, :].rearrange("p t d -> p (t d)"), acc_store[b]).then_inc(s_loaded[r], 16)

                def store(b, r):
                    sp.wait_ge(s_done, b + 1)
                    sp.dma_start(out_store[b], s_out[r][:, :, :].rearrange("p t d -> p (t d)")).then_inc(s_stored[r], 16)

                for r in range(RING):
                    load(r, r)
                with sp.Fori(0, NB // RING - 1) as turn:
                    for r in range(RING):
                        store(turn * RING + r, r)
                        load(turn * RING + r + RING, r)
                for r in range(RING):
                    store(NB - RING + r, r)
                for r in range(RING):
                    sp.wait_ge(s_stored[r], 16 * (NB // RING))

            @block_c.vector
            def _(dve):
                with dve.Fori(0, NB // RING) as turn:
                    for r in range(RING):
                        b = turn * RING + r
                        dve.wait_ge(s_loaded[r], 16 * (turn + 1))
                        for t in range(TILES):
                            nc.vector.bn_stats(stats[:, r, t, :], s_in[r][:, t, :]).then_inc(stats_done, 1)
                        wait_apart(dve, stats_done, TILES * (b + 1))
                        for t in range(TILES):
                            ins = nc.vector.bn_aggr(mean_var[:, r, t, :], stats[:, r, t, :])
                        ins.then_inc(mean_done, 1)

            @block_c.gpsimd
            def _(pool):
                G = nc.gpsimd
                G.memset(minus_half[:, :], -0.5).then_inc(half_made, 1)
                pool.wait_ge(half_made, 1)
                with pool.Fori(0, NB // RING) as turn:
                    for r in range(RING):
                        b = turn * RING + r
                        wait_apart(pool, mean_done, b + 1)
                        G.tensor_scalar(rstd[:, r, :], mean_var[:, r, :, 1], EPS, None, ALU.add).then_inc(norm_step, 1)
                        pool.wait_ge(norm_step, 3 * b + 1)
                        G.tensor_tensor(rstd[:, r, :], rstd[:, r, :], minus_half[:, :], ALU.pow).then_inc(norm_step, 1)
                        pool.wait_ge(norm_step, 3 * b + 2)
                        G.tensor_tensor(nshift[:, r, :], mean_var[:, r, :, 0], rstd[:, r, :], ALU.mult).then_inc(norm_step, 1)
                        wait_apart(pool, norm_step, 3 * b + 3)
                        G.tensor_scalar(nshift[:, r, :], nshift[:, r, :], -1.0, None, ALU.mult).then_inc(norm_ready, 1)

            @block_c.scalar
            def _(act):
                def body(turn, r):
                    b = turn * RING + r
                    act.wait_ge(norm_ready, b + 1)
                    if not isinstance(turn, int):
                        act.wait_ge(s_stored[r], 16 * turn)
                    for t in range(TILES):
                        ins = nc.scalar.activation(s_out[r][:, t, :], s_in[r][:, t, :], ACT.Identity,
                                                   bias=nshift[:, r, t:t + 1], scale=rstd[:, r, t:t + 1])
                    ins.then_inc(s_done, 1)

                for r in range(RING):
                    body(0, r)
                with act.Fori(1, NB // RING) as turn:
                    for r in range(RING):
                        body(turn, r)


def kernel(L0_attn_x, L0_attn_Wq, L0_attn_Wk, L0_attn_Wv, L0_attn_Wo, L0_attn_bo,
           L0_ffn_wr, L0_ffn_w1, L0_ffn_b1, L0_ffn_w2, L0_ffn_b2):
    import concourse.bacc as bacc
    from concourse.bass_utils import run_bass_kernel_spmd

    x = np.ascontiguousarray(L0_attn_x)
    NB, N, D = x.shape
    P, TILES = 128, N // 128
    E, FF = L0_ffn_b1.shape
    lay = np.ascontiguousarray
    arrays = {
        "x": x,
        "x_t": lay(x.reshape(NB, P, TILES, D).transpose(0, 3, 2, 1).reshape(NB, D, N)),
        "wq": lay(L0_attn_Wq), "wk": lay(L0_attn_Wk), "wv_t": lay(np.asarray(L0_attn_Wv).T), "wo": lay(L0_attn_Wo),
        "bo": lay(L0_attn_bo), "wr_t": lay(np.asarray(L0_ffn_wr).T),
        "w1": lay(L0_ffn_w1),
        "b1_t": lay(np.asarray(L0_ffn_b1).reshape(E, FF // P, P).transpose(2, 0, 1).reshape(P, -1)),
        "w2": lay(L0_ffn_w2),
        "b2_t": lay(np.asarray(L0_ffn_b2).reshape(E, D // P, P).transpose(2, 0, 1).reshape(P, -1)),
    }
    nc = bacc.Bacc("TRN2", target_bir_lowering=False, num_devices=1)
    args = [nc.dram_tensor(f"in_{n}", a.shape, mybir.dt.from_np(a.dtype), kind="ExternalInput").ap() for n, a in arrays.items()]
    out = nc.dram_tensor("out", (NB, N, D), mybir.dt.float32, kind="ExternalOutput").ap()
    build(nc, *args, out)
    r = run_bass_kernel_spmd(nc, [{f"in_{n}": a for n, a in arrays.items()}], core_ids=[0])
    return r.results[0]["out"]
```

```python
import numpy as np
import concourse.bass as bass
from concourse import mybir
from contextlib import ExitStack


def build(nc, x, x_t, wq, wk, wv_t, wo, bo, wr_t, w1, b1_t, w2, b2_t, out):
    F = mybir.dt.float32
    R = mybir.dt.float32r
    I = mybir.dt.int32
    ALU = mybir.AluOpType
    ACT = mybir.ActivationFunctionType
    X = mybir.AxisListType.X

    NB, N, D = x.shape
    E, _, FF = w1.shape
    P = 128
    T = NB * N
    TILES = N // P
    PAIRS = TILES // 2
    DK = D // P
    FT = FF // P
    CAP = max(8, int(T * 2 // E * 1.25))
    SLOTS = E * CAP
    TCOLS = SLOTS // P
    BLK = 512
    BT = BLK // P
    BLOCKS = CAP // BLK
    HEADS = 16
    CTX_SCALE = 1.0 / float(np.sqrt(D // HEADS)) / D
    EPS = 1e-5
    DROPPED = float(2 ** 23)
    assert CAP % (2 * BLK) == 0 and NB % 2 == 0 and E % 2 == 0 and TILES == 8 and DK == 2 and FT == 8

    x_rows = x.rearrange("b (p t) d -> b p (t d)", t=TILES)
    xt_rows = x_t.rearrange("b (k p) n -> b p k n", p=P)
    x1_dram = nc.dram_tensor("x1_rows", (T + BLK, D), F, kind="Internal").ap()
    acc_dram = nc.dram_tensor("sum_rows", (T + BLK, D), F, kind="Internal").ap()
    table_dram = nc.dram_tensor("slot_table", (SLOTS, 2), I, kind="Internal").ap()
    x1_store = x1_dram[0:T, :].rearrange("(b p t) d -> b p (t d)", p=P, t=TILES)
    acc_store = acc_dram[0:T, :].rearrange("(b p t) d -> b p (t d)", p=P, t=TILES)
    out_store = out.rearrange("b (p t) d -> b p (t d)", t=TILES)
    table_rows = table_dram.rearrange("(p c) w -> p (c w)", p=P)

    outer = ExitStack()
    with outer:
        def sem(name):
            return outer.enter_context(nc.semaphore(name))

        def sems(name, n):
            return [sem(f"{name}{i}") for i in range(n)]

        apart = sem("apart")

        def wait_apart(eng, which, value):
            eng.wait_ge(which, value)
            eng.sem_inc(apart, 1)

        def keep(name, shape, dt=F):
            return outer.enter_context(nc.sbuf_tensor(name, shape, dt))

        ident = keep("ident", [P, P])
        w_raw = keep("w_raw", [P, 2 * DK * FF])
        w_hi = [keep("w_hi0", [P, 2 * DK * FF], R), None]
        w_lo = [keep("w_lo0", [P, 2 * DK * FF], R), None]
        b1_sb = keep("b1_sb", [P, E * FT])
        b2_sb = keep("b2_sb", [P, E * DK])
        plan = keep("plan", [P, 2 * E + 1], I)
        W1 = DK * FF

        w_loaded = sem("w_loaded")
        w_split = sem("w_split")
        bias_loaded = sem("bias_loaded")

        def load_expert(sp, e):
            sp.dma_start(w_raw[:, 0:W1].rearrange("p (k f) -> p k f", k=DK),
                         w1[e, :, :].rearrange("(k p) f -> p k f", p=P)).then_inc(w_loaded, 16)
            sp.dma_start(w_raw[:, W1:2 * W1].rearrange("p (k d) -> p k d", k=FT),
                         w2[e, :, :].rearrange("(k p) d -> p k d", p=P)).then_inc(w_loaded, 16)

        with ExitStack() as phase:
            def sb(name, shape, dt=F):
                return phase.enter_context(nc.sbuf_tensor(name, shape, dt))

            def ps(name, shape):
                return phase.enter_context(nc.psum_tensor(name, shape, F))

            x_raw = [sb(f"x_raw{i}", [P, TILES, D]) for i in range(2)]
            xt_raw = [sb(f"xt_raw{i}", [P, DK * N]) for i in range(2)]
            x_hi, x_lo = sb("x_hi", [P, TILES, D], R), sb("x_lo", [P, TILES, D], R)
            xt_hi, xt_lo = sb("xt_hi", [P, DK * N], R), sb("xt_lo", [P, DK * N], R)
            wq_hi, wq_lo = sb("wq_hi", [P, DK, D], R), sb("wq_lo", [P, DK, D], R)
            wk_hi, wk_lo = sb("wk_hi", [P, DK, D], R), sb("wk_lo", [P, DK, D], R)
            wvo_hi, wvo_lo = sb("wvo_hi", [P, DK, D], R), sb("wvo_lo", [P, DK, D], R)
            wr_sb = sb("wr_sb", [P, DK, E])
            bo_sb = sb("bo_sb", [P, D])
            k_exp = sb("k_exp", [P, DK, N])
            q_exp = [sb(f"q_exp{i}", [P, TILES, D]) for i in range(2)]
            kt_hi, kt_lo = sb("kt_hi", [P, 2, 512], R), sb("kt_lo", [P, 2, 512], R)
            qt_hi, qt_lo = sb("qt_hi", [P, 2, 512], R), sb("qt_lo", [P, 2, 512], R)
            g_hi, g_lo = sb("g_hi", [P, DK, D], R), sb("g_lo", [P, DK, D], R)
            m_raw = sb("m_raw", [P, DK, D])
            m_hi, m_lo = sb("m_hi", [P, DK, D], R), sb("m_lo", [P, DK, D], R)
            x1_sb = [sb(f"x1_sb{i}", [P, TILES, D]) for i in range(2)]
            x1t = sb("x1t", [P, 2, 512])
            nk_max = sb("nk_max", [P, 2, DK])
            nq_max = sb("nq_max", [P, 2, TILES])
            zk, zq = sb("zk", [P, 2, DK]), sb("zq", [P, 2, TILES])
            rzk, rzq = sb("rzk", [P, DK]), sb("rzq", [P, TILES])
            stats = sb("stats", [P, TILES, 6])
            mean_var = sb("mean_var", [P, TILES, 2])
            rstd, nshift = sb("rstd", [P, TILES]), sb("nshift", [P, TILES])
            minus_half = sb("minus_half", [P, TILES])
            tri_f, ones_f = sb("tri_f", [P, P]), sb("ones_f", [P, P])
            ident_r, tri_r, ones_r = sb("ident_r", [P, P], R), sb("tri_r", [P, P], R), sb("ones_r", [P, P], R)
            logits = sb("logits", [P, TILES, E])
            second = sb("second", [P, TILES, E])
            eq = sb("eq", [P, TILES, E])
            score = sb("score", [P, TILES, E])
            pick = [sb(f"pick{i}", [P, TILES, E]) for i in range(2)]
            top = sb("top", [P, 2, TILES])
            best = sb("best", [P, TILES])
            mask = sb("mask", [P, TILES, E], R)
            mask_sum_f, mask_sum = sb("mask_sum_f", [P, E]), sb("mask_sum", [P, E], R)
            rank_base = sb("rank_base", [P, E])
            slot = sb("slot", [P, TILES, E])
            late = sb("late", [P, TILES, E])
            slot_f, slot_i = sb("slot_f", [P, 2, TILES]), sb("slot_i", [P, 2, TILES], I)
            slot_p, slot_c = sb("slot_p", [P, 2, TILES], I), sb("slot_c", [P, 2, TILES], I)
            gap, gap_exp = sb("gap", [P, TILES]), sb("gap_exp", [P, TILES])
            gate_sum = sb("gate_sum", [P, TILES])
            gates = sb("gates", [P, 2, TILES])
            token_id = sb("token_id", [P, TILES], I)
            order_w = sb("order_w", [P, E])
            slot_base = sb("slot_base", [P, E])
            ints = sb("ints", [P, 2, E], I)
            where = [sb(f"where{i}", [P, 2, TILES], I) for i in range(2)]
            entry = [sb(f"entry{i}", [P, 2, TILES, 2], I) for i in range(2)]
            pairs_f = sb("pairs_f", [P, 2 * E + 1])
            pad_entries = sb("pad_entries", [P, TCOLS, 2], I)
            zero_rows = sb("zero_rows", [P, D])
            w_in = x1_sb[1][:, :, :].rearrange("p (i k) d -> p i (k d)", i=4)

            k_ps = ps("k_ps", [P, N])
            gm_ps = ps("gm_ps", [P, DK, D])
            r_ps = ps("r_ps", [P, 512])
            l_ps = r_ps[:, 0:TILES * E].rearrange("p (t e) -> p t e", e=E)
            rank_ps = r_ps[:, 128:128 + TILES * E].rearrange("p (t e) -> p t e", e=E)
            total_ps = r_ps[:, 256:256 + E]
            o_ps = ps("o_ps", [P, 512])
            q_ps = ps("q_ps", [P, 512])
            t_ps = ps("t_ps", [P, 2, 512])

            consts_loaded = sem("consts_loaded")
            consts_made = sem("consts_made")
            consts_split = sem("consts_split")
            wvo_ready = sem("wvo_ready")
            pads_made, pads_stored = sem("pads_made"), sem("pads_stored")
            x_loaded, xt_loaded = sems("x_loaded", 2), sems("xt_loaded", 2)
            x_hi_done, x_lo_done = sem("x_hi_done"), sem("x_lo_done")
            xt_hi_done, xt_lo_done = sem("xt_hi_done"), sem("xt_lo_done")
            k_ready, k_max_done, k_exp_done = sem("k_ready"), sem("k_max_done"), sem("k_exp_done")
            q_ready, q_max_done, q_exp_done = sem("q_ready"), sem("q_max_done"), sem("q_exp_done")
            z_done = sem("z_done")
            kt_ready, kt_hi_done, kt_lo_done, kt_used = sem("kt_ready"), sem("kt_hi_done"), sem("kt_lo_done"), sem("kt_used")
            qt_ready, qt_hi_done, qt_lo_done = sem("qt_ready"), sem("qt_hi_done"), sem("qt_lo_done")
            g_hi_done, g_lo_done = sem("g_hi_done"), sem("g_lo_done")
            m_ready, m_raw_done, m_hi_done, m_lo_done = sem("m_ready"), sem("m_raw_done"), sem("m_hi_done"), sem("m_lo_done")
            o_ready, r_done, stats_done, mean_done = sem("o_ready"), sem("r_done"), sem("stats_done"), sem("mean_done")
            norm_step, norm_ready = sem("norm_step"), sem("norm_ready")
            x1_done, x1_stored = sem("x1_done"), sems("x1_stored", 2)
            x1t_ready, x1t_done = sem("x1t_ready"), sem("x1t_done")
            logits_ready, mask_ready, rank_ready = sem("logits_ready"), sem("mask_ready"), sem("rank_ready")
            gap_ready, gap_exp_done = sem("gap_ready"), sem("gap_exp_done")
            route_step, slots_ready = sem("route_step"), sem("slots_ready")
            entries_written = sems("entries_written", 2)
            const_step = sem("const_step")
            plan_step = sem("plan_step")

            def batches(eng, body, peeled=1):
                for pair in range(peeled):
                    for u in range(2):
                        body(pair, u, pair == 0 and u == 0, False)
                with eng.Fori(peeled, NB // 2 - 1) as pair:
                    for u in range(2):
                        body(pair, u, False, False)
                for u in range(2):
                    body(NB // 2 - 1, u, False, u == 1)

            block_a = phase.enter_context(nc.Block())

            @block_a.sync
            def _(sp):
                sp.dma_start(xt_raw[0][:, :].rearrange("p (k n) -> p k n", k=DK), xt_rows[0]).then_inc(xt_loaded[0], 16)
                for i, w in enumerate((wk, wq, wv_t, wo)):
                    sp.dma_start(w_in[:, i, :].rearrange("p (k d) -> p k d", k=DK),
                                 w.rearrange("(k p) d -> p k d", p=P)).then_inc(consts_loaded, 16)
                sp.dma_start(wr_sb[:, :, :], wr_t.rearrange("(k p) e -> p k e", p=P)).then_inc(consts_loaded, 16)
                sp.dma_start(bo_sb[:, :], bo.rearrange("(a d) -> a d", a=1).broadcast_to([P, D])).then_inc(consts_loaded, 16)
                sp.dma_start(x_raw[0][:, :, :].rearrange("p t d -> p (t d)"), x_rows[0]).then_inc(x_loaded[0], 16)
                sp.dma_start(xt_raw[1][:, :].rearrange("p (k n) -> p k n", k=DK), xt_rows[1]).then_inc(xt_loaded[1], 16)
                sp.dma_start(x_raw[1][:, :, :].rearrange("p t d -> p (t d)"), x_rows[1]).then_inc(x_loaded[1], 16)
                sp.wait_ge(pads_made, 2)
                sp.dma_start(table_rows, pad_entries[:, :, :].rearrange("p c w -> p (c w)")).then_inc(pads_stored, 16)
                for rows_dram in (x1_dram, acc_dram):
                    for t in range(BT):
                        sp.dma_start(rows_dram[T + t * P:T + (t + 1) * P, :], zero_rows[:, :]).then_inc(pads_stored, 16)
                load_expert(sp, 0)
                sp.dma_start(b1_sb[:, :], b1_t).then_inc(bias_loaded, 16)
                sp.dma_start(b2_sb[:, :], b2_t).then_inc(bias_loaded, 16)

                def body(pair, u, more=True):
                    b = pair * 2 + u
                    if more:
                        sp.wait_ge(xt_lo_done, b + 1)
                        sp.dma_start(xt_raw[u][:, :].rearrange("p (k n) -> p k n", k=DK), xt_rows[b + 2]).then_inc(xt_loaded[u], 16)
                        sp.wait_ge(r_done, (b + 1) * TILES)
                        sp.wait_ge(x_lo_done, b + 1)
                        sp.dma_start(x_raw[u][:, :, :].rearrange("p t d -> p (t d)"), x_rows[b + 2]).then_inc(x_loaded[u], 16)
                    sp.wait_ge(x1_done, b + 1)
                    sp.dma_start(x1_store[b], x1_sb[u][:, :, :].rearrange("p t d -> p (t d)")).then_inc(x1_stored[u], 16)
                    sp.dma_start(acc_store[b], x1_sb[u][:, :, :].rearrange("p t d -> p (t d)")).then_inc(x1_stored[u], 16)

                with sp.Fori(0, NB // 2 - 1) as pair:
                    for u in range(2):
                        body(pair, u)
                for u in range(2):
                    body(NB // 2 - 1, u, more=False)
                for u in range(2):
                    sp.wait_ge(x1_stored[u], 32 * (NB // 2))
                sp.wait_ge(pads_stored, 16 * (1 + 2 * BT))
                sp.wait_ge(bias_loaded, 32)

            @block_a.gpsimd
            def _(pool):
                count = [0]

                def made(ins):
                    count[0] += 1
                    ins.then_inc(const_step, 1)
                    pool.wait_ge(const_step, count[0])

                nc.gpsimd.memset(minus_half[:, :], -0.5)
                made(nc.gpsimd.memset(ident[:, :], 0.0))
                made(nc.gpsimd.affine_select(out=ident[:, :], in_=ident[:, :], compare_op=ALU.not_equal, fill=1.0,
                                             base=0, pattern=[[-1, P]], channel_multiplier=1))
                made(nc.gpsimd.memset(tri_f[:, :], 0.0))
                made(nc.gpsimd.affine_select(out=tri_f[:, :], in_=tri_f[:, :], compare_op=ALU.is_ge, fill=1.0,
                                             base=0, pattern=[[-1, P]], channel_multiplier=1))
                made(nc.gpsimd.memset(ones_f[:, :], 1.0))
                made(nc.gpsimd.memset(rank_base[:, :], 0.0))
                made(nc.gpsimd.iota(ints[:, 0, :], pattern=[[-1, E]], base=E, channel_multiplier=0))
                made(nc.gpsimd.iota(ints[:, 1, :], pattern=[[CAP, E]], base=0, channel_multiplier=0))
                made(nc.gpsimd.iota(token_id[:, :], pattern=[[1, TILES]], base=0, channel_multiplier=TILES))
                made(nc.gpsimd.tensor_copy(order_w[:, :], ints[:, 0, :]))
                made(nc.gpsimd.tensor_copy(slot_base[:, :], ints[:, 1, :]))
                nc.gpsimd.memset(zero_rows[:, :], 0.0).then_inc(pads_made, 1)
                made(nc.gpsimd.memset(pad_entries[:, :, :], 0))
                nc.gpsimd.iota(pad_entries[:, :, 0].rearrange("p (a t) -> p a t", t=BT), pattern=[[0, TCOLS // BT], [P, BT]], base=T, channel_multiplier=1).then_inc(pads_made, 1)
                nc.gpsimd.memset(best[:, :], 0.0).then_inc(consts_made, 1)

                def split_x(b, u, loads):
                    pool.wait_ge(x_hi_done, b + 1)
                    nc.gpsimd.tensor_tensor(x_lo[:, :, :], x_raw[u][:, :, :], x_hi[:, :, :].bitcast(F),
                                            ALU.subtract).then_inc(x_lo_done, 1)

                def scatter(b_prev, u_prev):
                    wait_apart(pool, slots_ready, b_prev + 1)
                    for t in range(TILES):
                        for c in range(2):
                            pool.indirect_dma_start(
                                out=table_dram, out_offset=bass.IndirectOffsetOnAxis(ap=where[u_prev][:, c, t:t + 1], axis=0),
                                in_=entry[u_prev][:, c, t, :], in_offset=None,
                                bounds_check=SLOTS - 1, oob_is_err=False).then_inc(entries_written[u_prev], 16)

                split_x(0, 0, 1)
                pool.wait_ge(pads_stored, 16 * (1 + 2 * BT))

                def body(pair, u, first, last):
                    b = pair * 2 + u
                    if not last:
                        split_x(b + 1, 1 - u, None)
                    if not first:
                        pool.wait_ge(x1_done, b)
                    wait_apart(pool, mean_done, b + 1)
                    nc.gpsimd.tensor_scalar(rstd[:, :], mean_var[:, :, 1], EPS, None, ALU.add).then_inc(norm_step, 1)
                    pool.wait_ge(norm_step, 3 * b + 1)
                    nc.gpsimd.tensor_tensor(rstd[:, :], rstd[:, :], minus_half[:, :], ALU.pow).then_inc(norm_step, 1)
                    pool.wait_ge(norm_step, 3 * b + 2)
                    nc.gpsimd.tensor_tensor(nshift[:, :], mean_var[:, :, 0], rstd[:, :], ALU.mult).then_inc(norm_step, 1)
                    wait_apart(pool, norm_step, 3 * b + 3)
                    nc.gpsimd.tensor_scalar(nshift[:, :], nshift[:, :], -1.0, None, ALU.mult).then_inc(norm_ready, 1)
                    if not first:
                        scatter(b - 1, 1 - u)

                batches(pool, body)
                scatter(NB - 1, 1)
                for u in range(2):
                    pool.wait_ge(entries_written[u], 16 * 2 * TILES * (NB // 2))

            @block_a.scalar
            def _(act):
                def split_xt_hi(b, pair, u, first):
                    act.wait_ge(xt_loaded[u], 16 * (pair + 1))
                    if not first:
                        act.wait_ge(q_ready, PAIRS * b)
                        act.wait_ge(xt_lo_done, b)
                    nc.scalar.activation(xt_hi[:, :], xt_raw[u][:, :], ACT.Copy).then_inc(xt_hi_done, 1)

                def split_x_hi(b, pair, u, first):
                    act.wait_ge(x_loaded[u], 16 * (pair + 1))
                    if not first:
                        act.wait_ge(kt_used, PAIRS * b)
                        act.wait_ge(x_lo_done, b)
                    nc.scalar.activation(x_hi[:, :, :], x_raw[u][:, :, :], ACT.Copy).then_inc(x_hi_done, 1)

                def evacuate_x1t(j, b_prev):
                    act.wait_ge(x1t_ready, PAIRS * b_prev + j + 1)
                    if j >= 2:
                        act.wait_ge(logits_ready, PAIRS * b_prev + j - 1)
                    nc.scalar.activation(x1t[:, j % 2, :], t_ps[:, j % 2, :], ACT.Copy).then_inc(x1t_done, 1)

                def route_exp(b_prev):
                    act.wait_ge(gap_ready, b_prev + 1)
                    nc.scalar.activation(gap_exp[:, :], gap[:, :], ACT.Exp).then_inc(gap_exp_done, 1)

                def k_softmax(b, u, o):
                    wait = DK * b + o + 1
                    act.wait_ge(k_max_done, wait)
                    nc.scalar.activation(k_exp[:, o, :], k_ps[:, :], ACT.Exp, bias=nk_max[:, u, o:o + 1],
                                         accum_out=zk[:, u, o:o + 1]).then_inc(k_exp_done, 1)

                def q_softmax(b, u, j):
                    act.wait_ge(q_max_done, PAIRS * b + j + 1)
                    for t in (2 * j, 2 * j + 1):
                        nc.scalar.activation(q_exp[u][:, t, :], q_ps[:, (t % 2) * D:(t % 2 + 1) * D], ACT.Exp,
                                             bias=nq_max[:, u, t:t + 1], accum_out=zq[:, u, t:t + 1]).then_inc(q_exp_done, 1)

                split_xt_hi(0, 0, 0, True)
                split_x_hi(0, 0, 0, True)
                for j in range(PAIRS):
                    if j % 2 == 1:
                        k_softmax(0, 0, j // 2)
                    q_softmax(0, 0, j)

                def body(pair, u, first, last):
                    b = pair * 2 + u
                    nxt = pair if u == 0 else pair + 1
                    for j in range(PAIRS):
                        act.wait_ge(kt_ready, PAIRS * b + j + 1)
                        if j >= 2 or not first:
                            act.wait_ge(kt_used, PAIRS * b + j - 1)
                        nc.scalar.activation(kt_hi[:, j % 2, :], t_ps[:, j % 2, :], ACT.Copy).then_inc(kt_hi_done, 1)
                    if not last:
                        split_xt_hi(b + 1, nxt, 1 - u, False)
                    act.wait_ge(kt_used, PAIRS * (b + 1))
                    if not first:
                        act.wait_ge(m_ready, b)
                    nc.scalar.activation(g_hi[:, :, :], gm_ps[:, :, :], ACT.Copy).then_inc(g_hi_done, 1)

                    def qt(j):
                        act.wait_ge(qt_ready, PAIRS * b + j + 1)
                        if j >= 2 or not first:
                            act.wait_ge(o_ready, PAIRS * b + j - 1)
                        nc.scalar.activation(qt_hi[:, j % 2, :], t_ps[:, j % 2, :], ACT.Copy).then_inc(qt_hi_done, 1)

                    qt(0)
                    qt(1)
                    if not first:
                        for j in range(PAIRS):
                            evacuate_x1t(j, b - 1)
                    if not last:
                        split_x_hi(b + 1, nxt, 1 - u, False)
                    for j in range(PAIRS):
                        if j < 2:
                            qt(j + 2)
                        if not last:
                            if j % 2 == 1:
                                k_softmax(b + 1, 1 - u, j // 2)
                            q_softmax(b + 1, 1 - u, j)
                        if j == 1 and not first:
                            route_exp(b - 1)
                batches(act, body)
                for j in range(PAIRS):
                    evacuate_x1t(j, NB - 1)
                route_exp(NB - 1)

            @block_a.vector
            def _(dve):
                dve.wait_ge(consts_loaded, 96)
                dve.wait_ge(consts_made, 1)
                for i, hi in enumerate((wk_hi, wq_hi)):
                    nc.vector.tensor_copy(hi[:, :, :].rearrange("p k d -> p (k d)"), w_in[:, i, :]).then_inc(consts_split, 1)
                for src, dst in ((ident, ident_r), (tri_f, tri_r), (ones_f, ones_r)):
                    nc.vector.tensor_copy(dst[:, :], src[:, :]).then_inc(consts_split, 1)
                dve.wait_ge(consts_split, 5)
                for i, (hi, lo) in enumerate(((wk_hi, wk_lo), (wq_hi, wq_lo))):
                    nc.vector.tensor_tensor(lo[:, :, :].rearrange("p k d -> p (k d)"), w_in[:, i, :],
                                            hi[:, :, :].rearrange("p k d -> p (k d)").bitcast(F),
                                            ALU.subtract).then_inc(consts_split, 1)

                def split_xt_lo(b, u, first):
                    dve.wait_ge(xt_hi_done, b + 1)
                    if not first:
                        dve.wait_ge(q_ready, PAIRS * b)
                    nc.vector.tensor_tensor(xt_lo[:, :], xt_raw[u][:, :], xt_hi[:, :].bitcast(F),
                                            ALU.subtract).then_inc(xt_lo_done, 1)

                split_xt_lo(0, 0, True)
                dve.wait_ge(wvo_ready, 1)
                wvo = t_ps[:, 0, :].rearrange("p (k d) -> p k d", k=DK)
                nc.vector.tensor_copy(wvo_hi[:, :, :], wvo).then_inc(consts_split, 1)
                dve.wait_ge(consts_split, 8)
                nc.vector.tensor_tensor(wvo_lo[:, :, :], wvo, wvo_hi[:, :, :].bitcast(F), ALU.subtract).then_inc(consts_split, 1)

                ROUTE_STEPS = 30

                def route(b, pair, u, part, state={}):
                    def step(ins):
                        ins.then_inc(route_step, 1)
                        state["k"] += 1
                        dve.wait_ge(route_step, ROUTE_STEPS * b + state["k"])

                    V = nc.vector
                    over_tiles = lambda a: a.rearrange("p (a e) -> p a e", a=1).broadcast_to([P, TILES, E])
                    over_experts = lambda a: a.rearrange("p (t a) -> p t a", a=1).broadcast_to([P, TILES, E])

                    def choose(c, src):
                        step(V.reduce_max(top[:, c, :], src[:, :, :], X))
                        step(V.tensor_tensor(eq[:, :, :], src[:, :, :], over_experts(top[:, c, :]), ALU.is_equal))
                        step(V.tensor_tensor(score[:, :, :], eq[:, :, :], over_tiles(order_w[:, :]), ALU.mult))
                        step(V.reduce_max(best[:, :], score[:, :, :], X))
                        step(V.tensor_tensor(pick[c][:, :, :], score[:, :, :], over_experts(best[:, :]), ALU.is_equal))

                    if part == 0:
                        state["k"] = 0
                        dve.wait_ge(logits_ready, PAIRS * (b + 1))
                        step(V.tensor_copy(logits[:, :, :], l_ps))
                        choose(0, logits)
                    elif part == 1:
                        step(V.scalar_tensor_tensor(second[:, :, :], pick[0][:, :, :], -3.0e38, logits[:, :, :],
                                                    ALU.mult, ALU.add))
                        choose(1, second)
                        step(V.tensor_tensor(mask[:, :, :], pick[0][:, :, :], pick[1][:, :, :], ALU.add))
                        V.tensor_tensor(gap[:, :], top[:, 1, :], top[:, 0, :], ALU.subtract).then_inc(gap_ready, 1)
                        step(V.tensor_reduce(mask_sum_f[:, :], mask[:, :, :].bitcast(F).rearrange("p t e -> p e t"), X, ALU.add))
                        V.tensor_copy(mask_sum[:, :], mask_sum_f[:, :]).then_inc(mask_ready, 1)
                    elif part == 2:
                        dve.wait_ge(gap_exp_done, b + 1)
                        step(V.tensor_scalar(gate_sum[:, :], gap_exp[:, :], 1.0, None, ALU.add))
                        step(V.reciprocal(gates[:, 0, :], gate_sum[:, :]))
                        step(V.tensor_tensor(gates[:, 1, :], gap_exp[:, :], gates[:, 0, :], ALU.mult))
                        dve.wait_ge(rank_ready, b + 1)
                        step(V.tensor_tensor(slot[:, :, :], rank_ps, over_tiles(rank_base[:, :]), ALU.add))
                        step(V.tensor_scalar(late[:, :, :], slot[:, :, :], float(CAP), DROPPED, ALU.is_ge, ALU.mult))
                        step(V.tensor_tensor(slot[:, :, :], slot[:, :, :], over_tiles(slot_base[:, :]), ALU.add))
                        step(V.tensor_tensor(slot[:, :, :], slot[:, :, :], late[:, :, :], ALU.add))
                        step(V.tensor_tensor(rank_base[:, :], rank_base[:, :], total_ps, ALU.add))
                    else:
                        for c in range(2):
                            step(V.tensor_tensor(pick[c][:, :, :], pick[c][:, :, :], slot[:, :, :], ALU.mult))
                            step(V.tensor_reduce(slot_f[:, c, :], pick[c][:, :, :], X, ALU.add))
                        step(V.tensor_copy(slot_i[:, :, :], slot_f[:, :, :]))
                        step(V.tensor_scalar(slot_p[:, :, :], slot_i[:, :, :], P - 1, None, ALU.bitwise_and))
                        step(V.tensor_scalar(slot_c[:, :, :], slot_i[:, :, :], P.bit_length() - 1, None,
                                             ALU.arith_shift_right))
                        if not (isinstance(pair, int) and pair == 0):
                            dve.wait_ge(entries_written[u], 16 * 2 * TILES * pair)
                        for c in range(2):
                            V.tensor_copy(entry[u][:, c, :, 0], token_id[:, :])
                        V.tensor_copy(entry[u][:, :, :, 1].bitcast(F), gates[:, :, :])
                        V.scalar_tensor_tensor(where[u][:, :, :], slot_p[:, :, :], float(TCOLS), slot_c[:, :, :],
                                               ALU.mult, ALU.add).then_inc(slots_ready, 1)
                        dve.wait_ge(slots_ready, b + 1)
                        step(V.tensor_scalar(token_id[:, :], token_id[:, :], N, None, ALU.add))
                        assert state["k"] == ROUTE_STEPS, state["k"]

                def k_maximum(b, u, o):
                    dve.wait_ge(k_ready, PAIRS * b + 2 * o + 2)
                    nc.vector.reduce_max(nk_max[:, u, o:o + 1], k_ps[:, :], X, negate=True).then_inc(k_max_done, 1)

                def q_maximum(b, u, j):
                    dve.wait_ge(q_ready, PAIRS * b + j + 1)
                    nc.vector.reduce_max(nq_max[:, u, 2 * j:2 * j + 2], q_ps[:, :].rearrange("p (t d) -> p t d", t=2), X,
                                         negate=True).then_inc(q_max_done, 1)

                def normalize(b, u, half):
                    dve.wait_ge(norm_ready, b + 1)
                    for t in range(half * TILES // 2, (half + 1) * TILES // 2):
                        ins = nc.vector.tensor_scalar(x1_sb[u][:, t, :], x1_sb[u][:, t, :], rstd[:, t:t + 1], nshift[:, t:t + 1],
                                                      ALU.mult, ALU.add)
                    if half:
                        ins.then_inc(x1_done, 1)

                for j in range(PAIRS):
                    if j % 2 == 1:
                        k_maximum(0, 0, j // 2)
                    q_maximum(0, 0, j)

                def body(pair, u, first, last):
                    b = pair * 2 + u
                    prev = pair if u == 1 else pair - 1
                    V = nc.vector

                    def kt(j):
                        dve.wait_ge(kt_hi_done, PAIRS * b + j + 1)
                        V.tensor_tensor(kt_lo[:, j % 2, :], t_ps[:, j % 2, :], kt_hi[:, j % 2, :].bitcast(F),
                                        ALU.subtract).then_inc(kt_lo_done, 1)

                    kt(0)
                    kt(1)
                    dve.wait_ge(k_exp_done, DK * (b + 1))
                    dve.wait_ge(q_exp_done, TILES * (b + 1))
                    V.reciprocal(rzk[:, :], zk[:, u, :]).then_inc(z_done, 1)
                    V.reciprocal(rzq[:, :], zq[:, u, :]).then_inc(z_done, 1)
                    dve.wait_ge(z_done, 3 * b + 2)
                    V.tensor_scalar(rzk[:, :], rzk[:, :], CTX_SCALE, None, ALU.mult).then_inc(z_done, 1)
                    kt(2)
                    if not first:
                        normalize(b - 1, 1 - u, 0)
                    kt(3)
                    if not first:
                        normalize(b - 1, 1 - u, 1)
                    dve.wait_ge(g_hi_done, b + 1)
                    V.tensor_tensor(g_lo[:, :, :], gm_ps[:, :, :], g_hi[:, :, :].bitcast(F), ALU.subtract).then_inc(g_lo_done, 1)

                    def qt(j):
                        dve.wait_ge(qt_hi_done, PAIRS * b + j + 1)
                        V.tensor_tensor(qt_lo[:, j % 2, :], t_ps[:, j % 2, :], qt_hi[:, j % 2, :].bitcast(F),
                                        ALU.subtract).then_inc(qt_lo_done, 1)

                    qt(0)
                    qt(1)
                    if not last:
                        split_xt_lo(b + 1, 1 - u, False)
                    dve.wait_ge(m_ready, b + 1)
                    dve.wait_ge(z_done, 3 * b + 3)
                    for o in range(DK):
                        V.scalar_tensor_tensor(m_raw[:, o, :], gm_ps[:, o, :], rzk[:, o:o + 1], bo_sb[:, :],
                                               ALU.mult, ALU.add).then_inc(m_raw_done, 1)
                    dve.wait_ge(m_raw_done, DK * (b + 1))
                    V.tensor_copy(m_hi[:, :, :], m_raw[:, :, :]).then_inc(m_hi_done, 1)
                    dve.wait_ge(m_hi_done, b + 1)
                    V.tensor_tensor(m_lo[:, :, :], m_raw[:, :, :], m_hi[:, :, :].bitcast(F), ALU.subtract).then_inc(m_lo_done, 1)

                    def residual(j):
                        dve.wait_ge(o_ready, PAIRS * b + j + 1)
                        if j == 0 and not (isinstance(pair, int) and pair == 0):
                            dve.wait_ge(x1_stored[u], 32 * pair)
                        for t in (2 * j, 2 * j + 1):
                            V.scalar_tensor_tensor(x1_sb[u][:, t, :], o_ps[:, (t % 2) * D:(t % 2 + 1) * D],
                                                   rzq[:, t:t + 1], x_raw[u][:, t, :], ALU.mult, ALU.add).then_inc(r_done, 1)
                        for t in (2 * j, 2 * j + 1):
                            dve.wait_ge(r_done, TILES * b + t + 1)
                            V.bn_stats(stats[:, t, :], x1_sb[u][:, t, :]).then_inc(stats_done, 1)

                    if not first:
                        route(b - 1, prev, 1 - u, 0)
                    for j in range(PAIRS):
                        if not last and j % 2 == 1:
                            k_maximum(b + 1, 1 - u, j // 2)
                        residual(j)
                        if j < 2:
                            qt(j + 2)
                        if not last:
                            q_maximum(b + 1, 1 - u, j)
                        if not first and j in (0, 2):
                            route(b - 1, prev, 1 - u, 1 + j // 2)
                    if not first:
                        dve.wait_ge(norm_ready, b)
                    wait_apart(dve, stats_done, TILES * (b + 1))
                    for t in range(TILES):
                        ins = V.bn_aggr(mean_var[:, t, :], stats[:, t, :])
                    ins.then_inc(mean_done, 1)
                    if not first:
                        route(b - 1, prev, 1 - u, 3)

                batches(dve, body, peeled=2)
                for half in range(2):
                    normalize(NB - 1, 1, half)
                for part in range(4):
                    route(NB - 1, NB // 2 - 1, 1, part)
                steps = 0

                def plan_next(ins):
                    nonlocal steps
                    ins.then_inc(plan_step, 1)
                    steps += 1
                    dve.wait_ge(plan_step, steps)

                V = nc.vector
                plan_next(V.memset(pairs_f[:, :], 0.0))
                plan_next(V.tensor_scalar(pairs_f[:, 0:E], rank_base[:, :], float(2 * BLK * 2), 2.0, ALU.is_gt, ALU.add))
                for k in range(3, BLOCKS // 2):
                    plan_next(V.tensor_scalar(slot_base[:, :], rank_base[:, :], float(2 * BLK * k), None, ALU.is_gt))
                    plan_next(V.tensor_tensor(pairs_f[:, 0:E], pairs_f[:, 0:E], slot_base[:, :], ALU.add))
                for e in range(E):
                    plan_next(V.tensor_tensor(pairs_f[:, E + e + 1:E + e + 2], pairs_f[:, E + e:E + e + 1],
                                              pairs_f[:, e:e + 1], ALU.add))
                plan_next(V.tensor_copy(plan[:, :], pairs_f[:, :]))
                dve.wait_ge(w_loaded, 32)
                nc.vector.tensor_copy(w_hi[0][:, :], w_raw[:, :]).then_inc(w_split, 1)
                dve.wait_ge(w_split, 1)
                nc.vector.tensor_tensor(w_lo[0][:, :], w_raw[:, :], w_hi[0][:, :].bitcast(F), ALU.subtract).then_inc(w_split, 1)
                dve.wait_ge(w_split, 2)

            @block_a.tensor
            def _(pe):
                def product(dst, a, b, start, stop):
                    nc.tensor.matmul(dst, a[0], b[0], start=start, stop=False)
                    nc.tensor.matmul(dst, a[0], b[1], start=False, stop=False)
                    return nc.tensor.matmul(dst, a[1], b[0], start=False, stop=stop)

                pe.wait_ge(consts_loaded, 96)
                wv_in = w_in[:, 2, :].rearrange("p (k d) -> p k d", k=DK)
                wo_in = w_in[:, 3, :].rearrange("p (k d) -> p k d", k=DK)
                for i in range(DK):
                    for o in range(DK):
                        ins = nc.tensor.matmul(t_ps[:, 0, i * D:(i + 1) * D], wv_in[:, o, i * P:(i + 1) * P], wo_in[:, o, :],
                                               start=(o == 0), stop=(o == DK - 1))
                ins.then_inc(wvo_ready, 1)
                pe.wait_ge(consts_split, 7)

                xt = [a[:, :].rearrange("p (k t n) -> p k t n", k=DK, t=TILES) for a in (xt_hi, xt_lo)]

                def k_logits(b, j, start_of_all):
                    o, h = j // 2, j % 2
                    if j == 0:
                        pe.wait_ge(xt_lo_done, b + 1)
                    if h == 0 and not (start_of_all and o == 0):
                        pe.wait_ge(k_exp_done, DK * b + o)
                    for i in range(3 * DK):
                        k, part = i // 3, i % 3
                        w = (wk_hi, wk_hi, wk_lo)[part]
                        v = (xt_hi, xt_lo, xt_hi)[part]
                        ins = nc.tensor.matmul(k_ps[:, h * 512:(h + 1) * 512], w[:, k, o * P:(o + 1) * P],
                                               v[:, k * N + h * 512:k * N + (h + 1) * 512], start=(i == 0), stop=(i == 3 * DK - 1))
                    ins.then_inc(k_ready, 1)

                def q_logits(b, j, start_of_all):
                    if not (start_of_all and j == 0):
                        pe.wait_ge(q_exp_done, TILES * b + 2 * j)
                    for i in range(2):
                        for k in range(DK):
                            t = 2 * j + i
                            ins = product(q_ps[:, i * D:(i + 1) * D], (xt[0][:, k, t, :], xt[1][:, k, t, :]),
                                          (wq_hi[:, k, :], wq_lo[:, k, :]), k == 0, k == DK - 1)
                    ins.then_inc(q_ready, 1)

                def transpose_x1(j, b_prev, u_prev):
                    pe.wait_ge(x1_done, b_prev + 1)
                    if j >= 2:
                        pe.wait_ge(x1t_done, PAIRS * b_prev + j - 1)
                    for i in range(2):
                        for k in range(DK):
                            c = (i * DK + k) * P
                            ins = nc.tensor.transpose(t_ps[:, j % 2, c:c + P], x1_sb[u_prev][:, 2 * j + i, k * P:(k + 1) * P], ident[:, :])
                    ins.then_inc(x1t_ready, 1)

                def router(j, b_prev):
                    pe.wait_ge(x1t_done, PAIRS * b_prev + j + 1)
                    for i in range(2):
                        for k in range(DK):
                            c = (i * DK + k) * P
                            ins = nc.tensor.matmul(l_ps[:, 2 * j + i, :], x1t[:, j % 2, c:c + P], wr_sb[:, k, :],
                                                   start=(k == 0), stop=(k == DK - 1))
                    ins.then_inc(logits_ready, 1)

                def rank(b_prev):
                    pe.wait_ge(mask_ready, b_prev + 1)
                    nc.tensor.matmul(total_ps, ones_r[:, :], mask_sum[:, :], start=True, stop=True)
                    nc.tensor.matmul(rank_ps, tri_r[:, :], mask_sum[:, :].rearrange("p (a e) -> p a e", a=1).broadcast_to([P, TILES, E]),
                                     start=True, stop=False)
                    for t in range(TILES - 1):
                        ins = nc.tensor.matmul(rank_ps[:, t + 1:TILES, :], ident_r[:, :],
                                               mask[:, t:t + 1, :].broadcast_to([P, TILES - 1 - t, E]),
                                               start=False, stop=(t == TILES - 2))
                    ins.then_inc(rank_ready, 1)

                def body(pair, u, first, last):
                    b = pair * 2 + u
                    def transpose_k(j):
                        if j == 0:
                            pe.wait_ge(k_exp_done, DK * (b + 1))
                        if j >= 2:
                            pe.wait_ge(kt_lo_done, PAIRS * b + j - 1)
                        elif not first:
                            pe.wait_ge(qt_lo_done, PAIRS * (b - 1) + j + 3)
                        for i in range(2):
                            t = 2 * j + i
                            for o in range(DK):
                                c = i * D + o * P
                                ins = nc.tensor.transpose(t_ps[:, j % 2, c:c + P], k_exp[:, o, t * P:(t + 1) * P], ident[:, :])
                        ins.then_inc(kt_ready, 1)

                    def context(j):
                        pe.wait_ge(kt_lo_done, PAIRS * b + j + 1)
                        if j == 0:
                            pe.wait_ge(x_lo_done, b + 1)
                            if not first:
                                pe.wait_ge(m_raw_done, DK * b)
                        for i in range(2):
                            t = 2 * j + i
                            for k in range(DK):
                                xs = [a[:, t, k * P:(k + 1) * P] for a in (x_hi, x_hi, x_lo)]
                                ks = [a[:, j % 2, i * D:(i + 1) * D] for a in (kt_hi, kt_lo, kt_hi)]
                                for part in range(3):
                                    ins = nc.tensor.matmul(gm_ps[:, k, :], xs[part], ks[part],
                                                           start=(t == 0 and k == 0 and part == 0),
                                                           stop=(t == TILES - 1 and k == DK - 1 and part == 2),
                                                           skip_group_check=True)
                        ins.then_inc(kt_used, 1)

                    def transpose_q(j):
                        if j == 0:
                            pe.wait_ge(q_exp_done, TILES * (b + 1))
                        if j < 2:
                            pe.wait_ge(kt_lo_done, PAIRS * b + j + 3)
                        elif first:
                            pe.wait_ge(qt_lo_done, PAIRS * b + j - 1)
                        else:
                            pe.wait_ge(x1t_done, PAIRS * (b - 1) + j + 1)
                        for i in range(2):
                            t = 2 * j + i
                            for o in range(DK):
                                c = i * D + o * P
                                ins = nc.tensor.transpose(t_ps[:, j % 2, c:c + P], q_exp[u][:, t, o * P:(o + 1) * P], ident[:, :])
                        ins.then_inc(qt_ready, 1)

                    def attend(j):
                        pe.wait_ge(qt_lo_done, PAIRS * b + j + 1)
                        if j == 0:
                            pe.wait_ge(m_lo_done, b + 1)
                        if j > 0 or not first:
                            pe.wait_ge(r_done, TILES * b + 2 * j)
                        for i in range(2):
                            for o in range(DK):
                                c = i * D + o * P
                                ins = product(o_ps[:, i * D:(i + 1) * D],
                                              (qt_hi[:, j % 2, c:c + P], qt_lo[:, j % 2, c:c + P]), (m_hi[:, o, :], m_lo[:, o, :]),
                                              o == 0, o == DK - 1)
                        ins.then_inc(o_ready, 1)

                    transpose_k(0)
                    transpose_k(1)
                    context(0)
                    transpose_k(2)
                    context(1)
                    transpose_k(3)
                    context(2)
                    context(3)
                    transpose_q(0)
                    transpose_q(1)
                    if not first:
                        pe.wait_ge(qt_lo_done, PAIRS * b + 1)
                        transpose_x1(0, b - 1, 1 - u)
                        pe.wait_ge(qt_lo_done, PAIRS * b + 2)
                        transpose_x1(1, b - 1, 1 - u)
                    pe.wait_ge(g_lo_done, b + 1)
                    if first:
                        pe.wait_ge(consts_split, 9)
                    for o in range(DK):
                        for i in range(DK):
                            ins = product(gm_ps[:, o, :], (g_hi[:, i, o * P:(o + 1) * P], g_lo[:, i, o * P:(o + 1) * P]),
                                          (wvo_hi[:, i, :], wvo_lo[:, i, :]), i == 0, i == DK - 1)
                    ins.then_inc(m_ready, 1)
                    if not first:
                        if not (isinstance(pair, int) and pair == 0):
                            pe.wait_ge(slots_ready, b - 1)
                        router(0, b - 1)
                        transpose_x1(2, b - 1, 1 - u)
                        router(1, b - 1)
                        transpose_x1(3, b - 1, 1 - u)
                        router(2, b - 1)
                        router(3, b - 1)
                    for j in range(PAIRS):
                        if not last:
                            k_logits(b + 1, j, False)
                        attend(j)
                        if j < 2:
                            transpose_q(j + 2)
                        if not last:
                            q_logits(b + 1, j, False)
                        if j == 1 and not first:
                            rank(b - 1)

                for j in range(PAIRS):
                    k_logits(0, j, True)
                    q_logits(0, j, True)
                batches(pe, body)
                b = NB - 1
                for j in range(2):
                    pe.wait_ge(qt_lo_done, PAIRS * b + j + 3)
                    transpose_x1(j, b, 1)
                pe.wait_ge(slots_ready, b)
                for j in range(PAIRS):
                    router(j, b)
                    if j < 2:
                        transpose_x1(j + 2, b, 1)
                rank(b)

        with ExitStack() as phase:
            def sb(name, shape, dt=F):
                return phase.enter_context(nc.sbuf_tensor(name, shape, dt))

            def ps(name, shape):
                return phase.enter_context(nc.psum_tensor(name, shape, F))

            w_hi[1] = sb("w_hi1", [P, 2 * DK * FF], R)
            w_lo[1] = sb("w_lo1", [P, 2 * DK * FF], R)
            table_in = sb("table_in", [P, TCOLS, 2], I)
            table = sb("table", [P, BT + TCOLS + 2 * BT, 2], I)
            pick_idx = [sb(f"pick_idx{i}", [P, BT], I) for i in range(2)]
            put_idx = sb("put_idx", [P, BT], I)
            put_gate = sb("put_gate", [P, BT])
            rows = [sb(f"rows{i}", [P, BT, D]) for i in range(2)]
            xt_hi = [sb(f"bt_hi{i}", [P, DK, BLK], R) for i in range(2)]
            xt_lo = [sb(f"bt_lo{i}", [P, DK, BLK], R) for i in range(2)]
            h_hi = sb("h_hi", [P, 4, BLK], R)
            h_lo = sb("h_lo", [P, 4, BLK], R)
            yt = sb("yt", [P, DK, BLK])
            y = sb("y", [P, BT, D])

            h_ps = ps("h_ps", [P, 4, BLK])
            y_ps = ps("y_ps", [P, DK, BLK])
            t_ps = ps("tb_ps", [P, 2 * BLK])

            table_loaded, table_padded = sem("table_loaded"), sem("table_padded")
            idx_ready, gathered = sems("idx_ready", 2), sems("gathered", 2)
            put_ready, added = sem("put_ready"), sem("added")
            xt_ready, bt_hi_done, bt_lo_done = sem("xt_ready"), sem("bt_hi_done"), sem("bt_lo_done")
            h_ready, gelu_done, h_hi_done, h_lo_done, h_used = (
                sem("h_ready"), sem("gelu_done"), sem("h_hi_done"), sem("h_lo_done"), sem("h_used"))
            yt_done, y_ready, y_done = sem("yt_done"), sem("y_ready"), sem("y_done")

            block_b = phase.enter_context(nc.Block())

            def pairs_of(eng, e):
                return (eng.value_load(plan[0:1, bass.ds(e, 1)], min_val=2, max_val=BLOCKS // 2),
                        eng.value_load(plan[0:1, bass.ds(e + E, 1)], min_val=0, max_val=(E - 1) * BLOCKS // 2))

            def all_pairs(eng):
                return eng.value_load(plan[0:1, 2 * E:2 * E + 1], min_val=2 * E, max_val=E * BLOCKS // 2)

            def experts(eng, body, between=None):
                with eng.Fori(0, E // 2) as half:
                    for eu in range(2):
                        if between is not None:
                            between(half, eu)
                        pairs, before = pairs_of(eng, half * 2 + eu)
                        with eng.Fori(0, pairs) as bp:
                            for bu in range(2):
                                body((before + bp) * 2 + bu, half * 2 + eu, eu, bu, before + bp)

            @block_b.sync
            def _(sp):
                sp.dma_start(table_in[:, :, :].rearrange("p c w -> p (c w)"), table_rows).then_inc(table_loaded, 16)
                with sp.Fori(0, E - 1) as e:
                    sp.wait_ge(w_split, 2 + 8 * 2 * e)
                    load_expert(sp, e + 1)

            @block_b.gpsimd
            def _(pool):
                G = nc.gpsimd
                G.memset(table[:, 0:BT, :], 0).then_inc(table_padded, 1)
                G.memset(table[:, BT + TCOLS:, :], 0).then_inc(table_padded, 1)
                pool.wait_ge(table_padded, 2)
                G.iota(table[:, 0:BT, 0], pattern=[[P, BT]], base=T, channel_multiplier=1).then_inc(table_padded, 1)
                G.iota(table[:, BT + TCOLS:, 0].rearrange("p (a t) -> p a t", t=BT), pattern=[[0, 2], [P, BT]], base=T, channel_multiplier=1).then_inc(table_padded, 1)
                pool.wait_ge(table_padded, 4)
                pool.wait_ge(table_loaded, 16)
                EC = CAP // P
                for e in range(E):
                    before = pool.value_load(plan[0:1, E + e:E + e + 1], min_val=0, max_val=e * BLOCKS // 2)
                    G.tensor_copy(table[:, bass.ds(before * (2 * BT) + BT, EC), :],
                                  table_in[:, e * EC:(e + 1) * EC, :]).then_inc(table_padded, 1)
                    pool.wait_ge(table_padded, 5 + e)

                def gather(n, u, uses):
                    G.tensor_copy(pick_idx[u][:, :], table[:, bass.ds(n * BT + BT, BT), 0]).then_inc(idx_ready[u], 1)
                    wait_apart(pool, idx_ready[u], uses + 1)
                    for t in range(BT):
                        pool.indirect_dma_start(
                            out=rows[u][:, t, :], out_offset=None, in_=x1_dram,
                            in_offset=bass.IndirectOffsetOnAxis(ap=pick_idx[u][:, t:t + 1], axis=0)).then_inc(gathered[u], 16)

                def put(n):
                    G.tensor_copy(put_idx[:, :], table[:, bass.ds(n * BT, BT), 0])
                    G.tensor_copy(put_gate[:, :], table[:, bass.ds(n * BT, BT), 1].bitcast(F)).then_inc(put_ready, 1)
                    pool.wait_ge(y_done, n + 1)
                    wait_apart(pool, put_ready, n + 1)
                    for t in range(BT):
                        pool.indirect_dma_start(
                            out=acc_dram, out_offset=bass.IndirectOffsetOnAxis(ap=put_idx[:, t:t + 1], axis=0),
                            in_=y[:, t, :], in_offset=None, compute_op=ALU.add).then_inc(added, 16)
                    pool.wait_ge(added, 16 * BT * (n + 1))

                gather(0, 0, 0)
                gather(1, 1, 0)

                def body(n, e, eu, bu, pair):
                    pool.wait_ge(xt_ready, n + 1)
                    gather(n + 2, bu, pair + 1)
                    put(n)

                experts(pool, body)
                total = all_pairs(pool)
                put(total * 2)
                for u in range(2):
                    pool.wait_ge(gathered[u], 16 * BT * (total + 1))

            @block_b.scalar
            def _(act):
                def split_hi(n, u):
                    act.wait_ge(xt_ready, n + 1)
                    nc.scalar.activation(xt_hi[u][:, :, :].rearrange("p k n -> p (k n)"), t_ps[:, :], ACT.Copy).then_inc(bt_hi_done, 1)

                split_hi(0, 0)

                def body(n, e, eu, bu, pair):
                    for f in range(FT):
                        c = f % 4
                        wait_apart(act, h_ready, n * FT + f + 1)
                        nc.scalar.activation(h_ps[:, c, :], h_ps[:, c, :], ACT.Gelu_apprx_tanh,
                                             bias=b1_sb[:, bass.ds(e * FT + f, 1)]).then_inc(gelu_done, 1)
                        act.wait_ge(gelu_done, n * FT + f + 1)
                        if f >= 4:
                            act.wait_ge(h_used, n * FT + f - 3)
                        nc.scalar.activation(h_hi[:, c, :], h_ps[:, c, :], ACT.Copy).then_inc(h_hi_done, 1)
                        if f == 5:
                            split_hi(n + 1, 1 - bu)
                    act.wait_ge(h_used, (n + 1) * FT)
                    wait_apart(act, y_ready, n + 1)
                    for k in range(DK):
                        ins = nc.scalar.activation(yt[:, k, :], y_ps[:, k, :], ACT.Identity,
                                                   bias=b2_sb[:, bass.ds(e * DK + k, 1)])
                    ins.then_inc(yt_done, 1)

                experts(act, body)

            @block_b.vector
            def _(dve):
                V = nc.vector
                V.memset(yt[:, :, :], 0.0).then_inc(yt_done, 1)

                def split_lo(n, u):
                    dve.wait_ge(bt_hi_done, n + 1)
                    V.tensor_tensor(xt_lo[u][:, :, :].rearrange("p k n -> p (k n)"), t_ps[:, :],
                                    xt_hi[u][:, :, :].rearrange("p k n -> p (k n)").bitcast(F), ALU.subtract).then_inc(bt_lo_done, 1)

                def scale_y(n):
                    dve.wait_ge(y_ready, n + 1)
                    dve.wait_ge(put_ready, n + 1)
                    for t in range(BT):
                        ins = V.tensor_scalar(y[:, t, :], t_ps[:, t * D:(t + 1) * D], put_gate[:, t:t + 1], None, ALU.mult)
                    ins.then_inc(y_done, 1)

                split_lo(0, 0)

                CH = 2 * DK * FF // 8

                def body(n, e, eu, bu, weights=False):
                    for f in range(FT):
                        c = f % 4
                        dve.wait_ge(h_hi_done, n * FT + f + 1)
                        V.tensor_tensor(h_lo[:, c, :], h_ps[:, c, :], h_hi[:, c, :].bitcast(F), ALU.subtract).then_inc(h_lo_done, 1)
                        if f == 3:
                            scale_y(n)
                        if f == 5:
                            split_lo(n + 1, 1 - bu)
                        if weights and f % 2 == 0:
                            piece = bu * 4 + f // 2
                            part = slice(piece * CH, (piece + 1) * CH)
                            dve.wait_ge(w_loaded, 32 * (e + 2))
                            V.tensor_copy(w_hi[1 - eu][:, part], w_raw[:, part]).then_inc(w_split, 1)
                            dve.wait_ge(w_split, 3 + e * 16 + piece * 2)
                            V.tensor_tensor(w_lo[1 - eu][:, part], w_raw[:, part], w_hi[1 - eu][:, part].bitcast(F),
                                            ALU.subtract).then_inc(w_split, 1)

                def expert(half, eu, last):
                    e = half * 2 + eu
                    pairs, before = pairs_of(dve, e)
                    for bu in range(2):
                        body(before * 2 + bu, e, eu, bu, not last)
                    with dve.Fori(1, pairs) as bp:
                        for bu in range(2):
                            body((before + bp) * 2 + bu, e, eu, bu)

                with dve.Fori(0, E // 2 - 1) as half:
                    for eu in range(2):
                        expert(half, eu, False)
                expert(E // 2 - 1, 0, False)
                expert(E // 2 - 1, 1, True)
                scale_y(all_pairs(dve) * 2)

            @block_b.tensor
            def _(pe):
                def transpose_rows(n, u, uses):
                    pe.wait_ge(gathered[u], 16 * BT * (uses + 1))
                    pe.wait_ge(y_done, n)
                    for k in range(DK):
                        for t in range(BT):
                            c = k * BLK + t * P
                            ins = nc.tensor.transpose(t_ps[:, c:c + P], rows[u][:, t, k * P:(k + 1) * P], ident[:, :])
                    ins.then_inc(xt_ready, 1)

                def transpose_y(n):
                    pe.wait_ge(bt_lo_done, n + 1)
                    for t in range(BT):
                        for k in range(DK):
                            c = t * D + k * P
                            ins = nc.tensor.transpose(t_ps[:, c:c + P], yt[:, k, t * P:(t + 1) * P], ident[:, :])
                    ins.then_inc(y_ready, 1)

                pe.wait_ge(gathered[0], 16 * BT)
                for k in range(DK):
                    for t in range(BT):
                        c = k * BLK + t * P
                        ins = nc.tensor.transpose(t_ps[:, c:c + P], rows[0][:, t, k * P:(k + 1) * P], ident[:, :])
                ins.then_inc(xt_ready, 1)

                def between(half, eu):
                    wait_apart(pe, w_split, 2 + 16 * (half * 2 + eu))

                def body(n, e, eu, bu, pair):
                    def up(f):
                        if f == 0:
                            pe.wait_ge(bt_lo_done, n + 1)
                        for i in range(3 * DK):
                            k, part = i // 3, i % 3
                            w = (w_hi, w_hi, w_lo)[part][eu]
                            v = (xt_hi, xt_lo, xt_hi)[part][bu]
                            c = k * FF + f * P
                            ins = nc.tensor.matmul(h_ps[:, f % 4, :], w[:, c:c + P], v[:, k, :], start=(i == 0), stop=(i == 3 * DK - 1))
                        ins.then_inc(h_ready, 1)

                    def down(f):
                        pe.wait_ge(h_lo_done, n * FT + f + 1)
                        if f == 0:
                            pe.wait_ge(yt_done, n + 1)
                        for k in range(DK):
                            for part in range(3):
                                w = (w_hi, w_hi, w_lo)[part][eu]
                                v = (h_hi, h_lo, h_hi)[part]
                                c = W1 + f * D + k * P
                                ins = nc.tensor.matmul(y_ps[:, k, :], w[:, c:c + P], v[:, f % 4, :],
                                                       start=(f == 0 and part == 0), stop=(f == FT - 1 and part == 2))
                        ins.then_inc(h_used, 1)

                    up(0)
                    up(1)
                    up(2)
                    down(0)
                    up(3)
                    down(1)
                    transpose_y(n)
                    up(4)
                    down(2)
                    transpose_rows(n + 1, 1 - bu, pair + bu)
                    up(5)
                    down(3)
                    up(6)
                    down(4)
                    up(7)
                    down(5)
                    down(6)
                    down(7)

                experts(pe, body, between)
                total = all_pairs(pe)
                pe.wait_ge(yt_done, total * 2 + 1)
                transpose_y(total * 2)

        with ExitStack() as phase:
            RING = 4
            s_in = [phase.enter_context(nc.sbuf_tensor(f"s_in{i}", [P, TILES, D], F)) for i in range(RING)]
            s_out = [phase.enter_context(nc.sbuf_tensor(f"s_out{i}", [P, TILES, D], F)) for i in range(RING)]
            stats = phase.enter_context(nc.sbuf_tensor("stats_c", [P, RING, TILES, 6], F))
            mean_var = phase.enter_context(nc.sbuf_tensor("mean_var_c", [P, RING, TILES, 2], F))
            rstd = phase.enter_context(nc.sbuf_tensor("rstd_c", [P, RING, TILES], F))
            nshift = phase.enter_context(nc.sbuf_tensor("nshift_c", [P, RING, TILES], F))
            minus_half = phase.enter_context(nc.sbuf_tensor("minus_half_c", [P, TILES], F))
            s_loaded, s_stored = sems("s_loaded", RING), sems("s_stored", RING)
            half_made, stats_done, mean_done = sem("half_made"), sem("stats_done_c"), sem("mean_done_c")
            norm_step, norm_ready, s_done = sem("norm_step_c"), sem("norm_ready_c"), sem("s_done")

            block_c = phase.enter_context(nc.Block())

            @block_c.sync
            def _(sp):
                def load(b, r):
                    sp.dma_start(s_in[r][:, :, :].rearrange("p t d -> p (t d)"), acc_store[b]).then_inc(s_loaded[r], 16)

                def store(b, r):
                    sp.wait_ge(s_done, b + 1)
                    sp.dma_start(out_store[b], s_out[r][:, :, :].rearrange("p t d -> p (t d)")).then_inc(s_stored[r], 16)

                for r in range(RING):
                    load(r, r)
                with sp.Fori(0, NB // RING - 1) as turn:
                    for r in range(RING):
                        store(turn * RING + r, r)
                        load(turn * RING + r + RING, r)
                for r in range(RING):
                    store(NB - RING + r, r)
                for r in range(RING):
                    sp.wait_ge(s_stored[r], 16 * (NB // RING))

            @block_c.vector
            def _(dve):
                with dve.Fori(0, NB // RING) as turn:
                    for r in range(RING):
                        b = turn * RING + r
                        dve.wait_ge(s_loaded[r], 16 * (turn + 1))
                        for t in range(TILES):
                            nc.vector.bn_stats(stats[:, r, t, :], s_in[r][:, t, :]).then_inc(stats_done, 1)
                        wait_apart(dve, stats_done, TILES * (b + 1))
                        for t in range(TILES):
                            ins = nc.vector.bn_aggr(mean_var[:, r, t, :], stats[:, r, t, :])
                        ins.then_inc(mean_done, 1)

            @block_c.gpsimd
            def _(pool):
                G = nc.gpsimd
                G.memset(minus_half[:, :], -0.5).then_inc(half_made, 1)
                pool.wait_ge(half_made, 1)
                with pool.Fori(0, NB // RING) as turn:
                    for r in range(RING):
                        b = turn * RING + r
                        wait_apart(pool, mean_done, b + 1)
                        G.tensor_scalar(rstd[:, r, :], mean_var[:, r, :, 1], EPS, None, ALU.add).then_inc(norm_step, 1)
                        pool.wait_ge(norm_step, 3 * b + 1)
                        G.tensor_tensor(rstd[:, r, :], rstd[:, r, :], minus_half[:, :], ALU.pow).then_inc(norm_step, 1)
                        pool.wait_ge(norm_step, 3 * b + 2)
                        G.tensor_tensor(nshift[:, r, :], mean_var[:, r, :, 0], rstd[:, r, :], ALU.mult).then_inc(norm_step, 1)
                        wait_apart(pool, norm_step, 3 * b + 3)
                        G.tensor_scalar(nshift[:, r, :], nshift[:, r, :], -1.0, None, ALU.mult).then_inc(norm_ready, 1)

            @block_c.scalar
            def _(act):
                def body(turn, r):
                    b = turn * RING + r
                    act.wait_ge(norm_ready, b + 1)
                    if not isinstance(turn, int):
                        act.wait_ge(s_stored[r], 16 * turn)
                    for t in range(TILES):
                        ins = nc.scalar.activation(s_out[r][:, t, :], s_in[r][:, t, :], ACT.Identity,
                                                   bias=nshift[:, r, t:t + 1], scale=rstd[:, r, t:t + 1])
                    ins.then_inc(s_done, 1)

                for r in range(RING):
                    body(0, r)
                with act.Fori(1, NB // RING) as turn:
                    for r in range(RING):
                        body(turn, r)


def kernel(L0_attn_x, L0_attn_Wq, L0_attn_Wk, L0_attn_Wv, L0_attn_Wo, L0_attn_bo,
           L0_ffn_wr, L0_ffn_w1, L0_ffn_b1, L0_ffn_w2, L0_ffn_b2):
    import concourse.bacc as bacc
    from concourse.bass_utils import run_bass_kernel_spmd

    x = np.ascontiguousarray(L0_attn_x)
    NB, N, D = x.shape
    P, TILES = 128, N // 128
    E, FF = L0_ffn_b1.shape
    lay = np.ascontiguousarray
    arrays = {
        "x": x,
        "x_t": lay(x.reshape(NB, P, TILES, D).transpose(0, 3, 2, 1).reshape(NB, D, N)),
        "wq": lay(L0_attn_Wq), "wk": lay(L0_attn_Wk), "wv_t": lay(np.asarray(L0_attn_Wv).T), "wo": lay(L0_attn_Wo),
        "bo": lay(L0_attn_bo), "wr_t": lay(np.asarray(L0_ffn_wr).T),
        "w1": lay(L0_ffn_w1),
        "b1_t": lay(np.asarray(L0_ffn_b1).reshape(E, FF // P, P).transpose(2, 0, 1).reshape(P, -1)),
        "w2": lay(L0_ffn_w2),
        "b2_t": lay(np.asarray(L0_ffn_b2).reshape(E, D // P, P).transpose(2, 0, 1).reshape(P, -1)),
    }
    nc = bacc.Bacc("TRN2", target_bir_lowering=False, num_devices=1)
    args = [nc.dram_tensor(f"in_{n}", a.shape, mybir.dt.from_np(a.dtype), kind="ExternalInput").ap() for n, a in arrays.items()]
    out = nc.dram_tensor("out", (NB, N, D), mybir.dt.float32, kind="ExternalOutput").ap()
    build(nc, *args, out)
    r = run_bass_kernel_spmd(nc, [{f"in_{n}": a for n, a in arrays.items()}], core_ids=[0])
    return r.results[0]["out"]
```
